# Optimizing a Trainium2 kernel written in Bass

```python
import numpy as np
import jax
import jax.numpy as jnp

def _softmax(x, axis=-1):
    return jax.nn.softmax(x, axis=axis)

def _gelu(x):
    return jax.nn.gelu(x, approximate=True)

def _silu(x):
    return jax.nn.silu(x)

def _sigmoid(x):
    return jax.nn.sigmoid(x)

def _layernorm(x, axis=-1, eps=1e-05):
    m = jnp.mean(x, axis=axis, keepdims=True)
    v = jnp.var(x, axis=axis, keepdims=True)
    return (x - m) / jnp.sqrt(v + eps)

def _scatter_add(tgt, idx, src, axis=0):
    return tgt.at[idx].add(src)

def _segment_sum(src, seg, n):
    return jax.ops.segment_sum(src, seg, n)
kernel_name = 'mk_xattn_ffn_d1_seqx_r8_cacaa6'

def setup_inputs(seed: int=0):
    np.random.seed(seed)
    _w = jnp.asarray

    def _rec_inputs():
        import jax
        import jax.numpy as jnp
        _rk = jax.random.key(seed)
        x = -0.0003929 + 0.9999 * jax.random.normal(jax.random.fold_in(_rk, 1), (128, 64, 128), jnp.float32)
        _lenS = 64 - jax.random.randint(jax.random.fold_in(_rk, 7), (128,), 0, max(1, 64 // 4) + 1, jnp.int32)
        _lenS2 = 64 - jax.random.randint(jax.random.fold_in(_rk, 8), (128,), 0, max(1, 64 // 4) + 1, jnp.int32)
        _ctx_1024P = jax.random.normal(jax.random.fold_in(_rk, 11), (128, 16, 128), jnp.float32)
        _ctx_1024c = jax.random.dirichlet(jax.random.fold_in(_rk, 511), 0.3 * jnp.ones((16,), jnp.float32), (128, 64))
        _ctx_1024t = jnp.einsum('bsk,bkd->bsd', _ctx_1024c, _ctx_1024P)
        _ctx_1024t = _ctx_1024t * jax.lax.rsqrt(jnp.mean(jnp.square(_ctx_1024t)) + 1e-12) * 0.953939
        ctx_1024 = 2.81802e-05 + 1.00001 * (_ctx_1024t + 0.3 * jax.random.normal(jax.random.fold_in(_rk, 611), (128, 64, 128), jnp.float32))
        return (x, ctx_1024)
    x, ctx_1024 = _rec_inputs()

    def _L0_xattn_setup():
        import jax, jax.numpy as jnp
        import numpy as np
        B_SZ, T_LEN, C_DIM = (4, 512, 128)

        def _wkv_scan(ek, v, ew):

            def step(carry, xt):
                A, Bd = carry
                ekt, vt = xt
                out = (A, Bd)
                A2 = ew * A + ekt * vt
                B2 = ew * Bd + ekt
                return ((A2, B2), out)
            init = (jnp.zeros_like(ek[:, 0]), jnp.zeros_like(ek[:, 0]))
            xs = (jnp.moveaxis(ek, 1, 0), jnp.moveaxis(v, 1, 0))
            _, (A, Bd) = jax.lax.scan(step, init, xs)
            return (jnp.moveaxis(A, 0, 1), jnp.moveaxis(Bd, 0, 1))

        def _birwkv(r, k, v, w, u):
            wc = w.reshape(-1)
            uc = u.reshape(-1)
            ew = jnp.exp(wc)
            ek = jnp.exp(k)
            Af, Bf = _wkv_scan(ek, v, ew)
            Ab, Bb = _wkv_scan(ek[:, ::-1], v[:, ::-1], ew)
            Ab = Ab[:, ::-1]
            Bb = Bb[:, ::-1]
            cur = jnp.exp(uc + k)
            wkv = (Af + Ab + cur * v) / (Bf + Bb + cur)
            return jax.nn.sigmoid(r) * wkv
        key = jax.random.key(seed)
        k1, k2, k3, k4, k5 = jax.random.split(key, 5)
        r = jax.random.normal(k1, (B_SZ, T_LEN, C_DIM), dtype=jnp.float32)
        k = jax.random.normal(k2, (B_SZ, T_LEN, C_DIM), dtype=jnp.float32)
        v = jax.random.normal(k3, (B_SZ, T_LEN, C_DIM), dtype=jnp.float32)
        w = -(0.3 + jax.random.uniform(k4, (1, 1, C_DIM), dtype=jnp.float32))
        u = jax.random.normal(k5, (1, 1, C_DIM), dtype=jnp.float32) * 0.1
        return {'r': r, 'k': k, 'v': v, 'w': w, 'u': u}
    _L0_xattn_all = _L0_xattn_setup()
    _L0_xattn_in = {k: v for k, v in _L0_xattn_all.items() if k in ('w', 'u')}
    del _L0_xattn_all

    def _L0_ffn_setup():
        import jax, jax.numpy as jnp
        import numpy as np
        D = 128
        E = 12
        HS = 2 * D
        HR = 3 * D
        TAU = 1.5

        def _geglu(h):
            a, g = jnp.split(h, 2, axis=-1)
            return a * jax.nn.gelu(g, approximate=False)
        key = jax.random.key(seed)
        ks = jax.random.split(key, 12)

        def xavier(k, shape):
            fan_in, fan_out = (shape[-2], shape[-1])
            lim = jnp.sqrt(6.0 / (fan_in + fan_out))
            return jax.random.uniform(k, shape, jnp.float32, -lim, lim)
        x = jax.random.normal(ks[0], (2, 128, D), jnp.float32)
        Ws1 = xavier(ks[1], (D, 2 * HS))
        bs1 = jnp.zeros((2 * HS,), jnp.float32)
        Ws2 = xavier(ks[2], (HS, D))
        bs2 = jnp.zeros((D,), jnp.float32)
        We1 = xavier(ks[3], (E, D, 2 * HR))
        be1 = jnp.zeros((E, 2 * HR), jnp.float32)
        We2 = xavier(ks[4], (E, HR, D))
        be2 = jnp.zeros((E, D), jnp.float32)
        Wr = xavier(ks[5], (D, E))
        br = jnp.zeros((E,), jnp.float32)
        return {'x': x, 'Ws1': Ws1, 'bs1': bs1, 'Ws2': Ws2, 'bs2': bs2, 'We1': We1, 'be1': be1, 'We2': We2, 'be2': be2, 'Wr': Wr, 'br': br}
    _L0_ffn_all = _L0_ffn_setup()
    _L0_ffn_in = {k: v for k, v in _L0_ffn_all.items() if k in ('Ws1', 'bs1', 'Ws2', 'bs2', 'We1', 'be1', 'We2', 'be2', 'Wr', 'br')}
    del _L0_ffn_all
    return {'x': x, 'ctx_1024': ctx_1024, 'L0_xattn_w': _L0_xattn_in['w'], 'L0_xattn_u': _L0_xattn_in['u'], 'L0_ffn_Ws1': _L0_ffn_in['Ws1'], 'L0_ffn_bs1': _L0_ffn_in['bs1'], 'L0_ffn_Ws2': _L0_ffn_in['Ws2'], 'L0_ffn_bs2': _L0_ffn_in['bs2'], 'L0_ffn_We1': _L0_ffn_in['We1'], 'L0_ffn_be1': _L0_ffn_in['be1'], 'L0_ffn_We2': _L0_ffn_in['We2'], 'L0_ffn_be2': _L0_ffn_in['be2'], 'L0_ffn_Wr': _L0_ffn_in['Wr'], 'L0_ffn_br': _L0_ffn_in['br']}

def reference(x, ctx_1024, L0_xattn_w, L0_xattn_u, L0_ffn_Ws1, L0_ffn_bs1, L0_ffn_Ws2, L0_ffn_bs2, L0_ffn_We1, L0_ffn_be1, L0_ffn_We2, L0_ffn_be2, L0_ffn_Wr, L0_ffn_br):
    import jax
    import jax.numpy as jnp

    def _L0_xattn_ref(r, k, v, w, u):
        import jax, jax.numpy as jnp
        import numpy as np
        B_SZ, T_LEN, C_DIM = (4, 512, 128)

        def _wkv_scan(ek, v, ew):

            def step(carry, xt):
                A, Bd = carry
                ekt, vt = xt
                out = (A, Bd)
                A2 = ew * A + ekt * vt
                B2 = ew * Bd + ekt
                return ((A2, B2), out)
            init = (jnp.zeros_like(ek[:, 0]), jnp.zeros_like(ek[:, 0]))
            xs = (jnp.moveaxis(ek, 1, 0), jnp.moveaxis(v, 1, 0))
            _, (A, Bd) = jax.lax.scan(step, init, xs)
            return (jnp.moveaxis(A, 0, 1), jnp.moveaxis(Bd, 0, 1))

        def _birwkv(r, k, v, w, u):
            wc = w.reshape(-1)
            uc = u.reshape(-1)
            ew = jnp.exp(wc)
            ek = jnp.exp(k)
            Af, Bf = _wkv_scan(ek, v, ew)
            Ab, Bb = _wkv_scan(ek[:, ::-1], v[:, ::-1], ew)
            Ab = Ab[:, ::-1]
            Bb = Bb[:, ::-1]
            cur = jnp.exp(uc + k)
            wkv = (Af + Ab + cur * v) / (Bf + Bb + cur)
            return jax.nn.sigmoid(r) * wkv
        return _birwkv(r, k, v, w, u)

    def _L0_ffn_ref(x, Ws1, bs1, Ws2, bs2, We1, be1, We2, be2, Wr, br):
        import jax, jax.numpy as jnp
        import numpy as np
        D = 128
        E = 12
        HS = 2 * D
        HR = 3 * D
        TAU = 1.5

        def _geglu(h):
            a, g = jnp.split(h, 2, axis=-1)
            return a * jax.nn.gelu(g, approximate=False)
        B, T, Dm = x.shape
        xf = x.reshape(-1, Dm)
        ys = _geglu(xf @ Ws1 + bs1) @ Ws2 + bs2
        logits = (xf @ Wr + br) / TAU
        top_val, top_idx = jax.lax.top_k(logits, 2)
        top_w = jax.nn.softmax(top_val, axis=-1)
        onehot = jax.nn.one_hot(top_idx, E, dtype=x.dtype)
        w = jnp.einsum('nke,nk->ne', onehot, top_w)
        h = jnp.einsum('nd,edh->enh', xf, We1) + be1[:, None, :]
        act = _geglu(h)
        yE = jnp.einsum('enh,ehd->end', act, We2) + be2[:, None, :]
        yr = jnp.einsum('end,ne->nd', yE, w)
        return (ys + yr).reshape(B, T, Dm)
    x = x + _L0_xattn_ref(_layernorm(x, axis=-1), ctx_1024, ctx_1024, L0_xattn_w, L0_xattn_u)
    x = x + _L0_ffn_ref(_layernorm(x, axis=-1), L0_ffn_Ws1, L0_ffn_bs1, L0_ffn_Ws2, L0_ffn_bs2, L0_ffn_We1, L0_ffn_be1, L0_ffn_We2, L0_ffn_be2, L0_ffn_Wr, L0_ffn_br)
    return x

_drawn_inputs = setup_inputs


def setup_inputs(seed=0):
    import zlib

    import numpy as np

    out = dict(_drawn_inputs(seed))
    spreads = {'L0_ffn_bs1': (0.0, 0.1),
     'L0_ffn_bs2': (0.0, 0.1),
     'L0_ffn_be1': (0.0, 0.1),
     'L0_ffn_be2': (0.0, 0.1),
     'L0_ffn_br': (0.0, 0.1)}
    factors = {'L0_xattn_u': 5.608}
    for name, (base, spread) in spreads.items():
        noise = np.random.default_rng([zlib.crc32(name.encode()), seed]).standard_normal(out[name].shape)
        drawn = base * np.exp(spread * noise) if base else spread * noise
        out[name] = jnp.asarray(drawn.astype(out[name].dtype))
    for name, factor in factors.items():
        out[name] = (out[name] * factor).astype(out[name].dtype)
    return out
```

```python
from contextlib import ExitStack

import concourse.bass as bass
from concourse import mybir

ALU = mybir.AluOpType
ACT = mybir.ActivationFunctionType
AX = mybir.AxisListType
F32 = mybir.dt.float32
F16 = mybir.dt.float16
BF16 = mybir.dt.bfloat16
I32 = mybir.dt.int32
U32 = mybir.dt.uint32

P = 128
EPS = 1e-5
TAU = 1.5
UP = 256.0
DOWN = 1.0 / UP


def xattn_ffn_kernel(nc, x, ctx_in, w, u, Ws1, bs1, Ws2, bs2, We1, be1, We2, be2, Wr, br, out):
    BATCH, T_LEN, C = x.shape
    E = Wr.shape[1]
    N = BATCH * T_LEN
    G = 1024
    J = G // P
    H = G // 2
    JH = H // P
    NG = N // G
    HS = Ws2.shape[0]
    HR = We2.shape[1]
    KS, KR = HS // P, HR // P
    S = 256
    NT = 2 * N // S + E - 1
    CAP = N + S
    ROW = P + 2
    PADROW = E * CAP
    NOWHERE = 1 << 20
    assert C == P and KR == 3 and KS == 2 and NG % 2 == 0 and E == 12 and H % T_LEN == 0

    xg_d = x.rearrange("b t c -> (b t) c").rearrange("(g j p) c -> g p j c", j=J, p=P)
    cg_d = ctx_in.rearrange("b t c -> (b t) c").rearrange("(g j p) c -> g p j c", j=J, p=P)
    og_d = out.rearrange("b t c -> (b t) c").rearrange("(g j p) c -> g p j c", j=J, p=P)
    sorted_d = nc.dram_tensor("sorted_rows", (E * CAP + S, ROW), F32, kind="Internal").ap()
    y_d = nc.dram_tensor("expert_out", (2 * N, P), F32, kind="Internal").ap()
    yg_d = y_d.rearrange("(g j p k) c -> g p j (k c)", j=J, p=P, k=2)

    with ExitStack() as ctx:
        def sb(name, shape, dt):
            return ctx.enter_context(nc.sbuf_tensor(name, shape, dt))

        def ps(name, shape, dt):
            return ctx.enter_context(nc.psum_tensor(name, shape, dt))

        def sem(name):
            return ctx.enter_context(nc.semaphore(name))

        acc = sb("acc", [P, NG * J, C], F32)
        w1h = sb("w1h", [P, E * 2 * HR], F16)
        w1l = sb("w1l", [P, E * 2 * HR], F16)
        w2 = sb("w2", [P, E * KR, C], F32)
        s1f = sb("s1f", [P, 2 * HS], F32)
        s1h = sb("s1h", [P, 2 * HS], F16)
        s1l = sb("s1l", [P, 2 * HS], F16)
        s2 = sb("s2", [P, KS, C], F32)
        wrf = sb("wrf", [P, E], F32)
        wrh = sb("wrh", [P, E], F16)
        wrl = sb("wrl", [P, E], F16)
        brb = sb("brb", [P, E], F32)
        NB = E * 2 * KR + 2 * KS + 2
        WROW, UROW = NB - 2, NB - 1
        vrow = sb("vrow", [NB, P], F32)
        vcol = sb("vcol", [P, NB], F32)
        vup = sb("vup", [P, NB], F32)
        b2s = sb("b2s", [3, (E + 1) * C], BF16)
        ewu = sb("ewu", [P, 2], F32)
        decay = sb("decay", [P, 2 * H + 1], F32)
        identf = sb("identf", [P, P], F32)
        identh = sb("identh", [P, P], F16)
        diagu = sb("diagu", [P, P], F32)
        before = sb("before", [P, P], BF16)
        ones = sb("ones", [P, P], BF16)
        epsc = sb("epsc", [P, 1], F32)
        sign = sb("sign", [P, 2 * J], F32)
        eidx = sb("eidx", [P, E], F32)
        ebase = sb("ebase", [P, E], F32)
        hist = sb("hist", [P, E], BF16)
        dest = sb("dest", [P, J, 2], F32)
        pad = sb("pad", [P, 2, ROW], F32)
        counts = sb("counts", [P, E], F32)
        tab = sb("tab", [1, 8, E], F32)
        tabi = sb("tabi", [1, 2, E], I32)
        tilev = sb("tilev", [1, 8, NT], F32)
        tileno = sb("tileno", [1, NT], F32)
        tileE = sb("tileE", [1, NT], I32)
        tileR = sb("tileR", [1, NT], I32)
        padat = sb("padat", [1, E], I32)

        ct = sb("ct", [P, 2, J, C], F32)
        ek = sb("ek", [P, 2, 2, 2, H], F32)
        fw = sb("fw", [P, 2, 2 * H + 1], F32)
        bw = sb("bw", [P, 2, 2 * H + 1], F32)
        nsig = sb("nsig", [P, 2, J, C], F32)
        dens = sb("dens", [P, H], F32)
        rcp = sb("rcp", [P, H], F32)
        lnl = sb("lnl", [P, 2 * J], F32)
        bns = sb("bns", [P, 2 * J, 6], F32)
        mv = sb("mv", [P, 2 * J, 2], F32)
        lnv = sb("lnv", [P, 2 * J], F32)
        lnr = sb("lnr", [P, 2 * J], F32)
        lnm = sb("lnm", [P, 2 * J], F32)
        lng = sb("lng", [P, 2 * J], F32)
        lnscale = sb("lnscale", [P, 2 * J], F32)
        lnbias = sb("lnbias", [P, 2 * J], F32)
        xn = sb("xn", [P, J, C], F32)
        rows = sb("rows", [P, 2, J, 2, ROW], F32)
        xT = sb("xT", [P, 2, 2, H], F16)
        gl = sb("gl", [P, H], F32)
        hid = sb("hid", [P, 2, KS, H], F32)
        wst = sb("wst", [P, 2, 2 * HR], F32)
        lg = sb("lg", [P, J, E], F32)
        top = sb("top", [P, J, 8], F32)
        topi = sb("topi", [P, J, 8], U32)
        oneh = sb("oneh", [P, J, 2, E], F32)
        both = sb("both", [P, J, E], BF16)
        seen = sb("seen", [P, E], F32)
        diff = sb("diff", [P, J], F32)
        ediff = sb("ediff", [P, J], F32)
        ediff1 = sb("ediff1", [P, J], F32)
        wfirst = sb("wfirst", [P, J], F32)
        place = sb("place", [P, J, E], F32)
        placed = sb("placed", [P, J, 2, E], F32)
        slot = sb("slot", [P, 2, J, 2], U32)

        b2w = (E + 1) * C
        b2f = hid[:, :, :, :].rearrange("p a k n -> p (a k n)")[0:1, 0:b2w]
        b2r = nsig[:, :, :, :].rearrange("p a j c -> p (a j c)")[0:1, 0:b2w]
        b2t = rows[:, :, :, :, :].rearrange("p a j m r -> p (a j m r)")[0:1, 0:b2w].bitcast(BF16)
        b2t = b2t.rearrange("p (a n) -> p a n", a=2)
        tile3 = bw[:, :, :].rearrange("p a n -> p (a n)")[0:1, 0:NT * E].rearrange("p (t e) -> p t e", e=E)
        tile3b = bw[:, :, :].rearrange("p a n -> p (a n)")[0:1, 1024:1024 + NT * E].rearrange("p (t e) -> p t e", e=E)
        assert NT * E <= 1024 and b2w <= 2048

        ctw = ct[:, :, :, :].rearrange("p a j c -> p (a j c)")
        tin = ctw[:, 0:3 * 2 * ROW].rearrange("p (s h r) -> p s h r", s=3, h=2)
        txT = ctw[:, 1024:1024 + 3 * S].bitcast(F16).rearrange("p (s l n) -> p s l n", s=3, l=2)
        fww = fw[:, :, :].rearrange("p a n -> p (a n)")
        tgl = fww[:, 0:KR * S].rearrange("p (k n) -> p k n", k=KR)
        bww = nsig[:, :, :, :].rearrange("p a j c -> p (a j c)")
        tyo = bww[:, 0:3 * S].rearrange("p (s h c) -> p s h c", s=3, h=2)
        ekw = ek[:, :, :, :, :].rearrange("p a h v n -> p (a h v n)")
        thid = ekw[:, 0:3 * KR * S].rearrange("p (s k n) -> p s k n", s=3, k=KR)
        ybuf = ekw.rearrange("p (s j k c) -> p s j k c", s=2, j=J, k=2)

        p_ct = ps("p_ct", [P, H], F32)
        p_num = ps("p_num", [P, H], F32)
        p_den = ps("p_den", [P, H], F32)
        p_xT = ps("p_xT", [P, 2, H], F16)
        p_rt = ps("p_rt", [P, 512], F32)
        p_g = ps("p_g", [P, H], F32)
        p_a = ps("p_a", [P, H], F32)
        p_y = ps("p_y", [P, H], F32)
        p_lg = p_rt[:, 0:J * E]
        p_pf = p_rt[:, 128:128 + J * E]
        p_cnt = p_rt[:, 256:256 + E]
        p_vec = p_rt[:, 384:384 + NB]
        p_tg = [p_ct, p_num, p_den]
        p_ta = [p_g, p_a, p_rt]
        p_tx = p_xT
        p_ty = p_y

        passed = sem("passed")
        x_in = [sem(f"x_in{k}") for k in range(2)]
        ctx_ld = [sem(f"ctx_ld{k}") for k in range(2)]
        w_ld = [sem(f"w_ld{k}") for k in range(2)]
        sw_in = sem("sw_in")
        w2_in = sem("w2_in")
        parts_in = sem("parts_in")
        pad_out = sem("pad_out")
        scat = [sem(f"scat{k}") for k in range(2)]
        pool_const = sem("pool_const")
        dve_const = sem("dve_const")
        act_const = sem("act_const")
        pe_const = sem("pe_const")
        ctxT_done = sem("ctxT_done")
        ek_done = sem("ek_done")
        ekv_done = sem("ekv_done")
        scan_done = sem("scan_done")
        swept = sem("swept")
        nd_done = sem("nd_done")
        den_done = sem("den_done")
        rden_done = sem("rden_done")
        newton = sem("newton")
        quo_done = sem("quo_done")
        x2_done = sem("x2_done")
        bn_done = sem("bn_done")
        mv_done = sem("mv_done")
        ln_step = sem("ln_step")
        guess_done = sem("guess_done")
        lnl_done = sem("lnl_done")
        dln_done = sem("dln_done")
        nsig_done = sem("nsig_done")
        xn_done = sem("xn_done")
        hi_done = sem("hi_done")
        lo_done = sem("lo_done")
        rows_done = sem("rows_done")
        xTp_done = sem("xTp_done")
        xT_done = sem("xT_done")
        lgp_done = sem("lgp_done")
        rt_step = sem("rt_step")
        both_done = sem("both_done")
        pf_done = sem("pf_done")
        diff_done = sem("diff_done")
        ediff_done = sem("ediff_done")
        meta_done = sem("meta_done")
        slot_done = sem("slot_done")
        upg_done = sem("upg_done")
        upa_done = sem("upa_done")
        gl_done = sem("gl_done")
        hid_done = sem("hid_done")
        yp_done = sem("yp_done")
        acc_done = sem("acc_done")
        whi_done = sem("whi_done")
        wlo_done = sem("wlo_done")
        cnt_done = sem("cnt_done")
        tab_step = sem("tab_step")
        tab_done = sem("tab_done")
        padded = sem("padded")
        t_in = [sem(f"t_in{k}") for k in range(3)]
        t_out = [sem(f"t_out{k}") for k in range(3)]
        txp_done = sem("txp_done")
        tx_done = sem("tx_done")
        tg_done = sem("tg_done")
        ta_done = sem("ta_done")
        tgl_done = sem("tgl_done")
        thid_done = sem("thid_done")
        typ_done = sem("typ_done")
        ty_done = sem("ty_done")
        y_in = [sem(f"y_in{k}") for k in range(2)]
        add1 = sem("add1")
        sum_done = sem("sum_done")
        out_done = sem("out_done")

        SW_LOADS, POOL_CONSTS, DVE_CONSTS, META = 16 * 10, 20, 11, 4
        LNS = 8

        def grp(i, c):
            return 2 * i + c

        def turn(i, c):
            return i + c // 2 + 1

        def steps(eng, body):
            for i in range(2):
                body(i, 0)
                body(i, 1)
            with eng.Fori(2, NG // 2) as i:
                body(i, 0)
                body(i, 1)
            body(NG // 2, 0)
            body(NG // 2, 1)

        def stages(i, c):
            if isinstance(i, int):
                s = grp(i, c)
                return s < NG, 1 <= s <= NG, 2 <= s <= NG + 1
            return True, True, True

        def ifat(eng, i, c, back, sm, value):
            if not isinstance(i, int) or grp(i, c) >= back:
                eng.wait_ge(sm, value)

        def alone(eng):
            eng.sem_inc(passed, 1)

        with nc.Block() as block:
            @block.sync
            def _(sp):
                def loads(i, c):
                    if not stages(i, c)[0]:
                        return
                    k, g = c % 2, grp(i, c)
                    ifat(sp, i, c, 2, ctxT_done, 2 * (g - 2) + 2)
                    sp.dma_start(ct[:, k, :, :], cg_d[g, :, :, :]).then_inc(ctx_ld[k], 16)
                    sp.dma_start(acc[:, bass.ds(g * J, J), :], xg_d[g, :, :, :]).then_inc(x_in[k], 16)

                def weights(i, c):
                    if not (stages(i, c)[0] and stages(i, c)[2]):
                        return
                    for k in range(2):
                        e = 2 * (grp(i, c) - 2) + k
                        ifat(sp, i, c, 3, wlo_done, e - 1)
                        sp.dma_start(wst[:, k, :], We1[e, :, :]).then_inc(w_ld[k], 16)

                sp.dma_start(vrow[0:E * 2 * KR, :], be1.rearrange("e (k p) -> (e k) p", p=P)).then_inc(sw_in, 16)
                sp.dma_start(vrow[E * 2 * KR:WROW, :], bs1.rearrange("(k p) -> k p", p=P)).then_inc(sw_in, 16)
                sp.dma_start(vrow[WROW:UROW, :], w[0, :, :]).then_inc(sw_in, 16)
                sp.dma_start(vrow[UROW:NB, :], u[0, :, :]).then_inc(sw_in, 16)
                sp.dma_start(b2f[:, 0:E * C], be2.rearrange("(a e) c -> a (e c)", a=1)).then_inc(sw_in, 16)
                sp.dma_start(b2f[:, E * C:], bs2.rearrange("(a c) -> a c", a=1)).then_inc(sw_in, 16)
                sp.dma_start(brb[:, :], br.partition_broadcast(P)).then_inc(sw_in, 16)
                sp.dma_start(wrf[:, :], Wr).then_inc(sw_in, 16)
                sp.dma_start(s1f[:, :], Ws1).then_inc(sw_in, 16)
                sp.dma_start(s2[:, :, :], Ws2.rearrange("(k p) d -> p k d", p=P)).then_inc(sw_in, 16)

                def body(i, c):
                    loads(i, c)
                    if isinstance(i, int) and grp(i, c) == 0:
                        sp.wait_ge(dve_const, DVE_CONSTS)
                        for m in range(2):
                            sp.dma_start(b2s[m + 1:m + 2, :], b2t[:, m, :]).then_inc(parts_in, 16)
                    weights(i, c)
                    if isinstance(i, int) and grp(i, c) == 1:
                        sp.dma_start(w2[:, :, :], We2.rearrange("e (k p) d -> p (e k) d", p=P)).then_inc(w2_in, 16)
                        sp.wait_ge(pool_const, POOL_CONSTS)
                        sp.dma_start(sorted_d[PADROW:PADROW + S, :].rearrange("(h p) r -> p h r", p=P),
                                     pad[:, :, :]).then_inc(pad_out, 16)
                steps(sp, body)
                sp.wait_ge(tab_done, 1)
                for e in range(E):
                    at = sp.value_load(padat[0:1, e:e + 1], min_val=e * CAP, max_val=e * CAP + N)
                    sp.dma_start(sorted_d[bass.ds(at, S), :].rearrange("(h p) r -> p h r", p=P),
                                 pad[:, :, :]).then_inc(padded, 16)
                sp.wait_ge(pad_out, 16)
                sp.wait_ge(padded, 16 * E)
                sp.wait_ge(w2_in, 16)
                for k in range(2):
                    sp.wait_ge(scat[k], 16 * 2 * J * (NG // 2))

            @block.gpsimd
            def _(pool):
                n = [0]

                def const(ins):
                    n[0] += 1
                    ins.then_inc(pool_const, 1)

                def behind(ins):
                    pool.wait_ge(pool_const, n[0])
                    const(ins())

                const(nc.gpsimd.memset(identf[:, :], 0.0))
                behind(lambda: nc.gpsimd.affine_select(out=identf[:, :], in_=identf[:, :], compare_op=ALU.not_equal,
                                                       fill=1.0, base=0, pattern=[[-1, P]], channel_multiplier=1))
                const(nc.gpsimd.memset(identh[:, :], 0.0))
                behind(lambda: nc.gpsimd.affine_select(out=identh[:, :], in_=identh[:, :], compare_op=ALU.not_equal,
                                                       fill=1.0, base=0, pattern=[[-1, P]], channel_multiplier=1))
                const(nc.gpsimd.memset(ones[:, :], 1.0))
                const(nc.gpsimd.memset(before[:, :], 1.0))
                behind(lambda: nc.gpsimd.affine_select(out=before[:, :], in_=before[:, :], compare_op=ALU.is_ge,
                                                       fill=0.0, base=-1, pattern=[[1, P]], channel_multiplier=-1))
                const(nc.gpsimd.memset(epsc[:, :], EPS))
                const(nc.gpsimd.memset(sign[:, 0:J], -1.0))
                const(nc.gpsimd.memset(sign[:, J:2 * J], 1.0))
                const(nc.gpsimd.memset(hist[:, :], 0.0))
                const(nc.gpsimd.iota(eidx[:, :], pattern=[[1, E]], base=0, channel_multiplier=0,
                                     allow_small_or_imprecise_dtypes=True))
                const(nc.gpsimd.iota(ebase[:, :], pattern=[[CAP, E]], base=0, channel_multiplier=0,
                                     allow_small_or_imprecise_dtypes=True))
                const(nc.gpsimd.iota(dest[:, :, :], pattern=[[2 * P, J], [1, 2]], base=0, channel_multiplier=2,
                                     allow_small_or_imprecise_dtypes=True))
                const(nc.gpsimd.iota(tileno[:, :], pattern=[[1, NT]], base=0, channel_multiplier=0,
                                     allow_small_or_imprecise_dtypes=True))
                const(nc.gpsimd.memset(pad[:, :, :], 0.0))
                behind(lambda: nc.gpsimd.memset(pad[:, :, P + 1:P + 2].bitcast(I32), NOWHERE))
                for h in range(2):
                    const(nc.gpsimd.memset(fw[:, h, 0:1], 0.0))
                const(nc.gpsimd.memset(bw[:, :, 2 * H:2 * H + 1], 0.0))
                assert n[0] == POOL_CONSTS

                def body(i, c):
                    begin, end, ffn = stages(i, c)
                    if begin or end:
                        s = grp(i, c)
                        lo, hi = (0 if begin else J), (2 * J if end else J)

                        def small(n, out, in0, in1, op=ALU.mult):
                            if not (isinstance(s, int) and s == 0 and n == 0):
                                pool.wait_ge(ln_step, LNS * s + n)
                                alone(pool)
                            if isinstance(in1, tuple):
                                ins = nc.gpsimd.tensor_scalar(out, in0, in1[0], in1[1], *in1[2:])
                            else:
                                ins = nc.gpsimd.tensor_tensor(out, in0, in1, op)
                            ins.then_inc(ln_step, 1)
                        pool.wait_ge(mv_done, s + 1)
                        alone(pool)
                        small(0, lnv[:, lo:hi], mv[:, lo:hi, 1], (EPS, None, ALU.add))
                        small(1, lnm[:, lo:hi], mv[:, lo:hi, 0], (-1.0, None, ALU.mult))
                        pool.wait_ge(guess_done, s + 1)
                        alone(pool)
                        small(2, lnr[:, lo:hi], lng[:, lo:hi], lng[:, lo:hi])
                        small(3, lnr[:, lo:hi], lnr[:, lo:hi], lnv[:, lo:hi])
                        small(4, lnr[:, lo:hi], lnr[:, lo:hi], (-0.5, 1.5, ALU.mult, ALU.add))
                        small(5, lnr[:, lo:hi], lnr[:, lo:hi], lng[:, lo:hi])
                        if not isinstance(i, int) or s >= 1:
                            pool.wait_ge(nsig_done, s if not isinstance(i, int) else min(s, NG))
                            alone(pool)
                        if not isinstance(i, int) or s >= 2:
                            pool.wait_ge(xn_done, s - 1)
                            alone(pool)
                        small(6, lnscale[:, lo:hi], lnr[:, lo:hi], sign[:, lo:hi])
                        small(7, lnbias[:, lo:hi], lnscale[:, lo:hi], lnm[:, lo:hi])
                    if ffn:
                        k, g = (c - 2) % 2, grp(i, c - 2)
                        pool.wait_ge(slot_done, g + 1)
                        alone(pool)
                        pool.wait_ge(meta_done, META * (g + 1))
                        alone(pool)
                        pool.wait_ge(rows_done, g + 1)
                        alone(pool)
                        for j in range(J):
                            for m in range(2):
                                pool.indirect_dma_start(
                                    out=sorted_d, out_offset=bass.IndirectOffsetOnAxis(ap=slot[:, k, j, m:m + 1], axis=0),
                                    in_=rows[:, k, j, m, :], in_offset=None).then_inc(scat[k], 16)
                steps(pool, body)

            @block.scalar
            def _(act):
                act.wait_ge(sw_in, SW_LOADS)
                nc.scalar.activation(s1h[:, :], s1f[:, :], ACT.Copy, scale=UP).then_inc(act_const, 1)
                nc.scalar.activation(wrh[:, :], wrf[:, :], ACT.Copy, scale=UP).then_inc(act_const, 1)
                act.wait_ge(pe_const, 1)
                nc.scalar.activation(vcol[:, :], p_vec, ACT.Copy).then_inc(act_const, 1)
                act.wait_ge(act_const, 3)
                nc.scalar.activation(ewu[:, :], vcol[:, WROW:NB], ACT.Exp).then_inc(act_const, 1)

                def exps(i, c, h):
                    g = grp(i, c)
                    act.wait_ge(ctxT_done, 2 * g + h + 1)
                    ifat(act, i, c, 2, nd_done, 2 * (g - 2) + h + 1)
                    nc.scalar.activation(ek[:, c % 2, h, 1, :], p_ct[:, :], ACT.Exp).then_inc(ek_done, 1)

                def reciprocal(i, c, h):
                    n = 2 * grp(i, c) + h
                    act.wait_ge(den_done, n + 1)
                    if not (isinstance(i, int) and n == 0):
                        act.wait_ge(x2_done, n)
                    nc.scalar.activation(rcp[:, :], dens[:, :], ACT.Ln).then_inc(dln_done, 1)
                    act.wait_ge(dln_done, n + 1)
                    nc.scalar.activation(rcp[:, :], rcp[:, :], ACT.Exp, scale=-1.0).then_inc(rden_done, 1)

                def body(i, c):
                    begin, end, ffn = stages(i, c)
                    if ffn:
                        g = grp(i, c - 2)
                        for h in range(2):
                            act.wait_ge(xTp_done, 2 * g + h + 1)
                            ifat(act, i, c, 3, upa_done, 4 * (g - 1) + 2 * h + 2)
                            ifat(act, i, c, 3, lgp_done, g)
                            nc.scalar.activation(xT[:, h, :, :], p_xT[:, :, :], ACT.Copy).then_inc(xT_done, 1)
                        for h in range(2):
                            for f in range(KS):
                                n = 4 * g + 2 * h + f
                                act.wait_ge(upg_done, n + 1)
                                if not (isinstance(i, int) and grp(i, c) == 2 and h == 0 and f == 0):
                                    act.wait_ge(hid_done, n)
                                nc.scalar.activation(gl[:, :], p_g[:, :], ACT.Gelu, scale=DOWN,
                                                     bias=vcol[:, E * 2 * KR + KS + f:E * 2 * KR + KS + f + 1]).then_inc(gl_done, 1)
                    nc.scalar.preload_act_table_set("natural_log_exp_and_others")
                    if begin:
                        exps(i, c, 0)
                    if end:
                        reciprocal(i, c - 1, 0)
                    if ffn:
                        g = grp(i, c - 2)
                        act.wait_ge(diff_done, g + 1)
                        ifat(act, i, c, 3, meta_done, META * g)
                        nc.scalar.activation(ediff[:, :], diff[:, :], ACT.Exp, scale=1.0 / TAU).then_inc(ediff_done, 1)
                    if begin:
                        exps(i, c, 1)
                    if end:
                        reciprocal(i, c - 1, 1)
                    if begin or end:
                        s = grp(i, c)
                        lo, hi = (0 if begin else J), (2 * J if end else J)
                        act.wait_ge(mv_done, s + 1)
                        ifat(act, i, c, 1, ln_step, LNS * s)
                        nc.scalar.activation(lnl[:, lo:hi], mv[:, lo:hi, 1], ACT.Ln, bias=epsc[:, 0:1]).then_inc(lnl_done, 1)
                        act.wait_ge(lnl_done, s + 1)
                        nc.scalar.activation(lng[:, lo:hi], lnl[:, lo:hi], ACT.Exp, scale=-0.5).then_inc(guess_done, 1)
                    if begin and ffn:
                        for k in range(2):
                            e = 2 * (grp(i, c) - 2) + k
                            act.wait_ge(w_ld[k], 16 * (grp(i, c) - 1))
                            alone(act)
                            nc.scalar.activation(w1h[:, bass.ds(e * 2 * HR, 2 * HR)], wst[:, k, :], ACT.Copy,
                                                 scale=UP).then_inc(whi_done, 1)
                    if begin or end:
                        act.wait_ge(ln_step, LNS * grp(i, c) + LNS)
                    if begin:
                        k, g = c % 2, grp(i, c)
                        ifat(act, i, c, 2, den_done, 2 * (g - 2) + 2)
                        alone(act)
                        for j in range(J):
                            ins = nc.scalar.activation(nsig[:, k, j, :], acc[:, g * J + j, :], ACT.Exp,
                                                       scale=lnscale[:, j:j + 1], bias=lnbias[:, j:j + 1])
                        ins.then_inc(nsig_done, 1)
                    if end:
                        k, g = (c - 1) % 2, grp(i, c - 1)
                        ifat(act, i, c, 2, lo_done, g)
                        alone(act)
                        for j in range(J):
                            ins = nc.scalar.activation(xn[:, j, :], acc[:, g * J + j, :], ACT.Identity,
                                                       scale=lnscale[:, J + j:J + j + 1], bias=lnbias[:, J + j:J + j + 1])
                        ins.then_inc(xn_done, 1)
                        act.wait_ge(xn_done, g + 1)
                        ifat(act, i, c, 3, xTp_done, 2 * (g - 2) + 2)
                        ifat(act, i, c, 3, scat[k], 16 * 2 * J * (turn(i, c - 1) - 1))
                        alone(act)
                        nc.scalar.activation(rows[:, k, :, 0, 0:C // 2].bitcast(F16), xn[:, :, :],
                                             ACT.Copy).then_inc(hi_done, 1)
                steps(act, body)

            @block.vector
            def _(dve):
                n = [0]

                def const(ins, wait=True):
                    n[0] += 1
                    ins.then_inc(dve_const, 1)
                    if wait:
                        dve.wait_ge(dve_const, n[0])

                dve.wait_ge(sw_in, SW_LOADS)
                dve.wait_ge(act_const, 4)
                dve.wait_ge(pool_const, POOL_CONSTS)
                const(nc.vector.tensor_copy(decay[:, :], ewu[:, 0:1].to_broadcast([P, 2 * H + 1])))
                const(nc.vector.memset(decay[:, 0:2 * H + 1:T_LEN], 0.0), False)
                const(nc.vector.tensor_scalar(diagu[:, :], identf[:, :], ewu[:, 1:2], None, ALU.mult), False)
                const(nc.vector.tensor_scalar(vup[:, :], vcol[:, :], UP, None, ALU.mult), False)
                const(nc.vector.scalar_tensor_tensor(s1l[:, :], s1f[:, :], UP, s1h[:, :], ALU.mult, ALU.subtract), False)
                const(nc.vector.scalar_tensor_tensor(wrl[:, :], wrf[:, :], UP, wrh[:, :], ALU.mult, ALU.subtract), False)
                const(nc.vector.tensor_scalar(b2r[:, :], b2f[:, :], UP, None, ALU.mult))
                const(nc.vector.tensor_copy(b2s[0:1, :], b2r[:, :]))
                const(nc.vector.tensor_tensor(b2f[:, :], b2r[:, :], b2s[0:1, :], ALU.subtract))
                const(nc.vector.tensor_copy(b2t[:, 0, :], b2f[:, :]))
                const(nc.vector.tensor_tensor(b2t[:, 1, :], b2f[:, :], b2t[:, 0, :], ALU.subtract))
                dve.wait_ge(parts_in, 32)
                assert n[0] == DVE_CONSTS

                def ekv(i, c, h):
                    g = grp(i, c)
                    dve.wait_ge(ek_done, 2 * g + h + 1)
                    nc.vector.tensor_tensor(ek[:, c % 2, h, 0, :], ek[:, c % 2, h, 1, :], p_ct[:, :],
                                            ALU.mult).then_inc(ekv_done, 1)

                def scan(i, c, h):
                    g = grp(i, c)
                    dve.wait_ge(ekv_done, 2 * g + h + 1)
                    ifat(dve, i, c, 1, nd_done, 2 * (g - 1) + h + 1)
                    src = ek[:, c % 2, h, :, :].rearrange("p v n -> p (v n)")
                    nc.vector.tensor_tensor_scan(fw[:, h, 1:2 * H + 1], decay[:, 0:2 * H], src, 0.0,
                                                 ALU.mult, ALU.add).then_inc(swept, 1)
                    nc.vector.tensor_tensor_scan(back(bw[:, h, 0:2 * H]), back(decay[:, 1:2 * H + 1]), back(src), 0.0,
                                                 ALU.mult, ALU.add).then_inc(swept, 1)
                    dve.wait_ge(swept, 4 * g + 2 * h + 2)
                    nc.vector.memset(fw[:, h, T_LEN:2 * H + 1:T_LEN], 0.0)
                    nc.vector.memset(bw[:, h, 0:2 * H:T_LEN], 0.0).then_inc(scan_done, 1)

                def back(a):
                    p, (_, m) = a.ap[0], a.ap[-1]
                    return bass.AP(a.tensor, a.offset + m - 1, [list(p), [-1, m]])

                def den(i, c, h):
                    k, g = c % 2, grp(i, c)
                    dve.wait_ge(nd_done, 2 * g + h + 1)
                    dve.wait_ge(nsig_done, g + 1)
                    if not (isinstance(i, int) and g == 0 and h == 0):
                        dve.wait_ge(x2_done, 2 * g + h)
                    nc.vector.scalar_tensor_tensor(dens[:, :], nsig[:, k, h * JH:(h + 1) * JH, :].rearrange("p j c -> p (j c)"),
                                                   1.0, p_den[:, :], ALU.add, ALU.mult).then_inc(den_done, 1)

                def add(i, c, h):
                    g = grp(i, c)
                    n = 2 * g + h
                    dve.wait_ge(rden_done, n + 1)
                    nc.vector.tensor_tensor(dens[:, :], dens[:, :], rcp[:, :], ALU.mult).then_inc(newton, 1)
                    nc.vector.tensor_tensor(rcp[:, :], p_num[:, :], rcp[:, :], ALU.mult).then_inc(quo_done, 1)
                    dve.wait_ge(quo_done, n + 1)
                    nc.vector.scalar_tensor_tensor(rcp[:, :], dens[:, :], 2.0, rcp[:, :], ALU.subtract, ALU.mult).then_inc(newton, 1)
                    dve.wait_ge(newton, 2 * n + 2)
                    at = acc[:, bass.ds(g * J + h * JH, JH), :].rearrange("p j c -> p (j c)")
                    nc.vector.tensor_tensor(at, at, rcp[:, :], ALU.subtract).then_inc(x2_done, 1)

                def geglu(i, c, h, f):
                    g = grp(i, c)
                    n = 4 * g + 2 * h + f
                    dve.wait_ge(upa_done, n + 1)
                    dve.wait_ge(gl_done, n + 1)
                    ifat(dve, i, c, 1, yp_done, 2 * (g - 1) + h + 1)
                    nc.vector.scalar_tensor_tensor(hid[:, h, f, :], p_a[:, :], vup[:, E * 2 * KR + f:E * 2 * KR + f + 1],
                                                   gl[:, :], ALU.add, ALU.mult).then_inc(hid_done, 1)

                def addffn(i, c, h):
                    g = grp(i, c)
                    dve.wait_ge(yp_done, 2 * g + h + 1)
                    at = acc[:, bass.ds(g * J + h * JH, JH), :].rearrange("p j c -> p (j c)")
                    nc.vector.scalar_tensor_tensor(at, p_y[:, :], DOWN, at, ALU.mult, ALU.add).then_inc(acc_done, 1)

                def route(i, c):
                    g = grp(i, c)
                    dve.wait_ge(lgp_done, g + 1)
                    ifat(dve, i, c, 1, rt_step, 5 * g)
                    ifat(dve, i, c, 1, tab_step, 5 * g)
                    ifat(dve, i, c, 1, meta_done, META * g)
                    nc.vector.scalar_tensor_tensor(lg[:, :, :], p_lg.rearrange("p (j e) -> p j e", e=E), DOWN,
                                                   brb[:, None, :].to_broadcast([P, J, E]), ALU.mult, ALU.add).then_inc(rt_step, 1)
                    dve.wait_ge(rt_step, 5 * g + 1)
                    alone(dve)
                    for j in range(J):
                        ins = nc.vector.max(top[:, j, :], lg[:, j, :])
                    ins.then_inc(rt_step, 1)
                    dve.wait_ge(rt_step, 5 * g + 2)
                    alone(dve)
                    for j in range(J):
                        ins = nc.vector.max_index(topi[:, j, :], top[:, j, :], lg[:, j, :])
                    ifat(dve, i, c, 1, ediff_done, g)
                    nc.vector.tensor_tensor(diff[:, :], top[:, :, 1], top[:, :, 0], ALU.subtract).then_inc(diff_done, 1)
                    ins.then_inc(rt_step, 1)
                    dve.wait_ge(rt_step, 5 * g + 3)
                    nc.vector.tensor_tensor(oneh[:, :, :, :], topi[:, :, 0:2, None].to_broadcast([P, J, 2, E]),
                                            eidx[:, None, None, :].to_broadcast([P, J, 2, E]),
                                            ALU.is_equal).then_inc(rt_step, 1)
                    dve.wait_ge(rt_step, 5 * g + 4)
                    ifat(dve, i, c, 1, pf_done, g)
                    nc.vector.tensor_tensor(both[:, :, :], oneh[:, :, 0, :], oneh[:, :, 1, :], ALU.add).then_inc(both_done, 1)

                def assign(i, c):
                    k, g = c % 2, grp(i, c)
                    meta = rows[:, k, :, :, :]
                    dve.wait_ge(pf_done, g + 1)
                    nc.vector.tensor_tensor(place[:, :, :], p_pf.rearrange("p (j e) -> p j e", e=E),
                                            ebase[:, None, :].to_broadcast([P, J, E]), ALU.add).then_inc(rt_step, 1)
                    nc.vector.tensor_reduce(seen[:, :], both[:, :, :].rearrange("p j e -> p e j"), AX.X, ALU.add).then_inc(tab_step, 1)
                    dve.wait_ge(ediff_done, g + 1)
                    nc.vector.tensor_scalar(ediff1[:, :], ediff[:, :], 1.0, None, ALU.add).then_inc(tab_step, 1)
                    ifat(dve, i, c, 2, scat[k], 16 * 2 * J * (turn(i, c) - 1))
                    nc.vector.tensor_copy(meta[:, :, :, P + 1].bitcast(I32), dest[:, :, :]).then_inc(meta_done, 1)
                    dve.wait_ge(rt_step, 5 * g + 5)
                    nc.vector.tensor_tensor(placed[:, :, :, :], oneh[:, :, :, :],
                                            place[:, :, None, :].to_broadcast([P, J, 2, E]), ALU.mult).then_inc(tab_step, 1)
                    dve.wait_ge(tab_step, 5 * g + 2)
                    nc.vector.tensor_tensor(hist[:, :], hist[:, :], seen[:, :], ALU.add).then_inc(tab_step, 1)
                    nc.vector.reciprocal(wfirst[:, :], ediff1[:, :]).then_inc(meta_done, 1)
                    dve.wait_ge(meta_done, META * g + 2)
                    nc.vector.tensor_scalar(dest[:, :, :], dest[:, :, :], 2.0 * G, None, ALU.add).then_inc(tab_step, 1)
                    dve.wait_ge(tab_step, 5 * g + 3)
                    with nc.allow_low_precision(reason="a row's number, a whole number below 2**24"):
                        nc.vector.tensor_reduce(slot[:, k, :, :], placed[:, :, :, :], AX.X, ALU.add).then_inc(slot_done, 1)
                    nc.vector.tensor_scalar(meta[:, :, 0, P], wfirst[:, :], DOWN, None, ALU.mult).then_inc(meta_done, 1)
                    nc.vector.scalar_tensor_tensor(meta[:, :, 1, P], wfirst[:, :], DOWN, ediff[:, :],
                                                   ALU.mult, ALU.mult).then_inc(meta_done, 1)

                def stats(i, c, first, at):
                    g = grp(i, c)
                    for j in range(J):
                        ins = nc.vector.bn_stats(bns[:, at + j, :], acc[:, g * J + j, :])
                    return ins

                def body(i, c):
                    begin, end, ffn = stages(i, c)
                    s = grp(i, c)
                    if begin or end:
                        ifat(dve, i, c, 1, mv_done, s)
                    if begin:
                        dve.wait_ge(x_in[c % 2], 16 * turn(i, c))
                        alone(dve)
                        stats(i, c, True, 0).then_inc(bn_done, 1)
                    if ffn:
                        geglu(i, c - 2, 0, 0)
                        route(i, c - 2)
                        geglu(i, c - 2, 0, 1)
                        geglu(i, c - 2, 1, 0)
                        addffn(i, c - 2, 0)
                        geglu(i, c - 2, 1, 1)
                    if end:
                        den(i, c - 1, 0)
                    if begin:
                        ekv(i, c, 0)
                        scan(i, c, 0)
                    if end:
                        add(i, c - 1, 0)
                    if ffn:
                        addffn(i, c - 2, 1)
                    if begin:
                        ekv(i, c, 1)
                    if ffn:
                        assign(i, c - 2)
                    if end:
                        den(i, c - 1, 1)
                    if begin:
                        scan(i, c, 1)
                    if end:
                        add(i, c - 1, 1)
                        dve.wait_ge(x2_done, 2 * grp(i, c - 1) + 2)
                        alone(dve)
                        stats(i, c - 1, False, J).then_inc(bn_done, 1)
                    if begin or end:
                        if not isinstance(i, int):
                            dve.wait_ge(bn_done, 2 * s + 1)
                        else:
                            dve.wait_ge(bn_done, min(s + 1, NG) + min(s, NG))
                        ifat(dve, i, c, 1, ln_step, LNS * s)
                        alone(dve)
                        lo, hi = (0 if begin else J), (2 * J if end else J)
                        for j in range(lo, hi):
                            ins = nc.vector.bn_aggr(mv[:, j, :], bns[:, j, :])
                        ins.then_inc(mv_done, 1)
                    if begin and ffn:
                        for k in range(2):
                            e = 2 * (s - 2) + k
                            dve.wait_ge(whi_done, e + 1)
                            nc.vector.scalar_tensor_tensor(w1l[:, bass.ds(e * 2 * HR, 2 * HR)], wst[:, k, :], UP,
                                                           w1h[:, bass.ds(e * 2 * HR, 2 * HR)],
                                                           ALU.mult, ALU.subtract).then_inc(wlo_done, 1)
                    if end:
                        k, g = (c - 1) % 2, grp(i, c - 1)
                        dve.wait_ge(hi_done, g + 1)
                        nc.vector.tensor_tensor(rows[:, k, :, 0, C // 2:C].bitcast(F16), xn[:, :, :],
                                                rows[:, k, :, 0, 0:C // 2].bitcast(F16), ALU.subtract).then_inc(lo_done, 1)
                        dve.wait_ge(lo_done, g + 1)
                        ifat(dve, i, c, 3, scat[k], 16 * 2 * J * (turn(i, c - 1) - 1))
                        nc.vector.tensor_copy(rows[:, k, :, 1, 0:C], rows[:, k, :, 0, 0:C]).then_inc(rows_done, 1)
                steps(dve, body)

                n = [5 * NG]

                def link(ins):
                    n[0] += 1
                    ins.then_inc(tab_step, 1)
                    dve.wait_ge(tab_step, n[0])

                def row(k):
                    return tab[:, k, :]

                def trow(k):
                    return tilev[:, k, :]

                dve.wait_ge(cnt_done, 1)
                link(nc.vector.tensor_copy(counts[:, :], p_cnt))
                link(nc.vector.tensor_scalar(tabi[:, 0, :], counts[0:1, :], float(S - 1), None, ALU.add))
                link(nc.vector.tensor_scalar(tabi[:, 1, :], tabi[:, 0, :], S.bit_length() - 1, None,
                                             ALU.logical_shift_right))
                link(nc.vector.tensor_copy(row(0), tabi[:, 1, :]))
                link(nc.vector.memset(row(2), 1.0))
                link(nc.vector.tensor_tensor_scan(row(1), row(2), row(0), 0.0, ALU.mult, ALU.add))
                link(nc.vector.tensor_tensor(row(3), row(1), row(0), ALU.subtract))
                link(nc.vector.scalar_tensor_tensor(row(4), row(3), -float(S), ebase[0:1, :], ALU.mult, ALU.add))
                link(nc.vector.tensor_tensor(tile3[:, :, :], tileno[:, :, None].to_broadcast([1, NT, E]),
                                             tab[:, 1:2, :].to_broadcast([1, NT, E]), ALU.is_ge))
                link(nc.vector.tensor_reduce(trow(0), tile3[:, :, :], AX.X, ALU.add))
                link(nc.vector.tensor_scalar(tileE[:, :], trow(0), float(E - 1), None, ALU.min))
                link(nc.vector.tensor_tensor(tile3b[:, :, :], eidx[0:1, None, :].to_broadcast([1, NT, E]),
                                             tilev[:, 0, :, None].to_broadcast([1, NT, E]), ALU.is_equal))
                link(nc.vector.tensor_tensor(tile3[:, :, :], tile3b[:, :, :], tab[:, 4:5, :].to_broadcast([1, NT, E]),
                                             ALU.mult))
                link(nc.vector.tensor_reduce(trow(1), tile3[:, :, :], AX.X, ALU.add))
                link(nc.vector.tensor_scalar(trow(2), tileno[:, :], float(S), None, ALU.mult))
                link(nc.vector.tensor_tensor(trow(3), trow(1), trow(2), ALU.add))
                link(nc.vector.tensor_scalar(trow(4), trow(2), -1.0, float(PADROW), ALU.mult, ALU.add))
                link(nc.vector.tensor_scalar(trow(5), trow(0), float(E), None, ALU.is_ge))
                link(nc.vector.tensor_tensor(trow(6), trow(4), trow(5), ALU.mult))
                link(nc.vector.tensor_tensor(tileR[:, :], trow(3), trow(6), ALU.add))
                nc.vector.tensor_tensor(padat[:, :], counts[0:1, :], ebase[0:1, :], ALU.add).then_inc(tab_done, 1)

            @block.tensor
            def _(pe):
                pe.wait_ge(sw_in, SW_LOADS)
                pe.wait_ge(pool_const, POOL_CONSTS)
                nc.tensor.transpose(p_vec, vrow[:, :], identf[0:NB, 0:NB]).then_inc(pe_const, 1)
                pe.wait_ge(act_const, 4)
                pe.wait_ge(dve_const, DVE_CONSTS)
                pe.wait_ge(parts_in, 32)

                def ctxT(i, c, h):
                    k, g = c % 2, grp(i, c)
                    if h == 0:
                        pe.wait_ge(ctx_ld[k], 16 * turn(i, c))
                    if not (isinstance(i, int) and g == 0 and h == 0):
                        pe.wait_ge(ekv_done, 2 * g + h)
                    for j in range(JH):
                        ins = nc.tensor.transpose(p_ct[:, j * P:(j + 1) * P], ct[:, k, h * JH + j, :], identf[:, :])
                    ins.then_inc(ctxT_done, 1)

                def numden(i, c, h):
                    k, g = c % 2, grp(i, c)
                    pe.wait_ge(scan_done, 2 * g + h + 1)
                    if not (isinstance(i, int) and g == 0 and h == 0):
                        pe.wait_ge(quo_done, 2 * g + h)
                    for v, bank in ((1, p_den), (0, p_num)):
                        for j in range(JH):
                            to = bank[:, j * P:(j + 1) * P]
                            a = v * H + j * P
                            nc.tensor.matmul(to, fw[:, h, a:a + P], identf[:, :], start=True, stop=False)
                            nc.tensor.matmul(to, bw[:, h, a + 1:a + 1 + P], identf[:, :], start=False, stop=False)
                            ins = nc.tensor.matmul(to, ek[:, k, h, v, j * P:(j + 1) * P], diagu[:, :],
                                                   start=False, stop=True)
                    ins.then_inc(nd_done, 1)

                def turnx(i, c, h):
                    k, g = c % 2, grp(i, c)
                    pe.wait_ge(lo_done, g + 1)
                    if not (isinstance(i, int) and g == 0 and h == 0):
                        pe.wait_ge(xT_done, 2 * g + h)
                    for l in range(2):
                        for j in range(JH):
                            ins = nc.tensor.transpose(
                                p_xT[:, l, j * P:(j + 1) * P],
                                rows[:, k, h * JH + j, 0, l * (C // 2):(l + 1) * (C // 2)].bitcast(F16), identh[:, :])
                    ins.then_inc(xTp_done, 1)

                def router(i, c):
                    g = grp(i, c)
                    pe.wait_ge(xT_done, 2 * g + 2)
                    ifat(pe, i, c, 1, slot_done, g)
                    for j in range(J):
                        xh = xT[:, j // JH, 0, (j % JH) * P:(j % JH + 1) * P]
                        xl = xT[:, j // JH, 1, (j % JH) * P:(j % JH + 1) * P]
                        to = p_lg[:, j * E:(j + 1) * E]
                        nc.tensor.matmul(to, xh, wrh[:, :], start=True, stop=False)
                        nc.tensor.matmul(to, xh, wrl[:, :], start=False, stop=False)
                        ins = nc.tensor.matmul(to, xl, wrh[:, :], start=False, stop=True)
                    ins.then_inc(lgp_done, 1)

                def prefix(i, c):
                    g = grp(i, c)
                    pe.wait_ge(both_done, g + 1)
                    ifat(pe, i, c, 1, slot_done, g)
                    nc.tensor.matmul(p_pf, before[:, :], both[:, :, :].rearrange("p j e -> p (j e)"), start=True, stop=False)
                    for j in range(J - 1):
                        nc.tensor.matmul(p_pf[:, (j + 1) * E:J * E], ones[:, :],
                                         both[:, j:j + 1, :].to_broadcast([P, J - 1 - j, E]), start=False, stop=False)
                    nc.tensor.matmul(p_pf, ones[:, :], hist[:, None, :].to_broadcast([P, J, E]),
                                     start=False, stop=True).then_inc(pf_done, 1)

                def up(i, c, h, f):
                    g = grp(i, c)
                    n = 4 * g + 2 * h + f
                    pe.wait_ge(xT_done, 2 * g + h + 1)
                    for bank, off, done, used in ((p_g, HS, upg_done, gl_done), (p_a, 0, upa_done, hid_done)):
                        if not (isinstance(i, int) and g == 0 and h == 0 and f == 0):
                            pe.wait_ge(used, n)
                        cols = slice(off + f * P, off + (f + 1) * P)
                        nc.tensor.matmul(bank[:, :], s1h[:, cols], xT[:, h, 0, :], start=True, stop=False)
                        nc.tensor.matmul(bank[:, :], s1h[:, cols], xT[:, h, 1, :], start=False, stop=False)
                        nc.tensor.matmul(bank[:, :], s1l[:, cols], xT[:, h, 0, :], start=False, stop=True).then_inc(done, 1)

                def down(i, c, h):
                    g = grp(i, c)
                    pe.wait_ge(hid_done, 4 * g + 2 * h + 2)
                    if not (isinstance(i, int) and g == 0 and h == 0):
                        pe.wait_ge(acc_done, 2 * g + h)
                    for j in range(JH):
                        to = p_y[:, j * P:(j + 1) * P]
                        for f in range(KS):
                            nc.tensor.matmul(to, hid[:, h, f, j * P:(j + 1) * P], s2[:, f, :], start=(f == 0), stop=False)
                        ins = nc.tensor.matmul(to, ones[0:3, :], b2s[:, E * C:(E + 1) * C], start=False, stop=True)
                    ins.then_inc(yp_done, 1)

                def body(i, c):
                    begin, end, ffn = stages(i, c)
                    if ffn:
                        turnx(i, c - 2, 0)
                        turnx(i, c - 2, 1)
                        up(i, c - 2, 0, 0)
                        router(i, c - 2)
                        up(i, c - 2, 0, 1)
                    if begin:
                        ctxT(i, c, 0)
                    if ffn:
                        up(i, c - 2, 1, 0)
                        down(i, c - 2, 0)
                        up(i, c - 2, 1, 1)
                    if end:
                        numden(i, c - 1, 0)
                    if ffn:
                        down(i, c - 2, 1)
                    if begin:
                        ctxT(i, c, 1)
                    if ffn:
                        prefix(i, c - 2)
                    if end:
                        numden(i, c - 1, 1)
                steps(pe, body)
                pe.wait_ge(tab_step, 5 * NG)
                nc.tensor.matmul(p_cnt, ones[:, :], hist[:, :], start=True, stop=True).then_inc(cnt_done, 1)

        def tiles(eng, body):
            for c in range(3):
                body(0, c, True, False)
            with eng.Fori(1, NT // 3 - 1) as i:
                for c in range(3):
                    body(i, c, False, False)
            for c in range(3):
                body(NT // 3 - 1, c, False, c == 2)
        assert NT % 3 == 0

        with nc.Block() as block:
            @block.sync
            def _(sp):
                def body(i, c, first, last):
                    t = 3 * i + c
                    at = sp.value_load(tileR[0:1, bass.ds(t, 1)], min_val=0, max_val=PADROW)
                    if not first:
                        sp.wait_ge(t_out[c], 32 * i)
                    sp.dma_start(tin[:, c, :, :], sorted_d[bass.ds(at, S), :].rearrange("(h p) r -> p h r", p=P)
                                 ).then_inc(t_in[c], 16)
                tiles(sp, body)

            @block.tensor
            def _(pe):
                def turnx(i, c):
                    t = 3 * i + c
                    pe.wait_ge(t_in[c % 3], 16 * (i + c // 3 + 1))
                    if not (isinstance(i, int) and t == 0):
                        pe.wait_ge(tx_done, t)
                    for l in range(2):
                        for h in range(2):
                            ins = nc.tensor.transpose(p_tx[:, 0, l * S + h * P:l * S + (h + 1) * P],
                                                      tin[:, c % 3, h, l * (C // 2):(l + 1) * (C // 2)].bitcast(F16),
                                                      identh[:, :])
                    ins.then_inc(txp_done, 1)

                def up(i, c, k, e, first):
                    t = 3 * i + c
                    if k == 0:
                        pe.wait_ge(tx_done, t + 1)
                    if not (first and c == 0):
                        pe.wait_ge(thid_done, 3 * (t - 1) + k + 1)
                    xh, xl = txT[:, c, 0, :], txT[:, c, 1, :]
                    for bank, off, done in ((p_tg[k], KR + k, tg_done), (p_ta[k], k, ta_done)):
                        to = bank[:, 0:S]
                        cols = bass.ds(e * (2 * HR) + off * P, P)
                        nc.tensor.matmul(to, w1h[:, cols], xh, start=True, stop=False)
                        nc.tensor.matmul(to, w1h[:, cols], xl, start=False, stop=False)
                        nc.tensor.matmul(to, w1l[:, cols], xh, start=False, stop=True).then_inc(done, 1)

                def down(i, c, e):
                    t = 3 * i + c
                    pe.wait_ge(thid_done, 3 * t + 3)
                    if not (isinstance(i, int) and t == 0):
                        pe.wait_ge(ty_done, t)
                    for h in range(2):
                        to = p_ty[:, h * P:(h + 1) * P]
                        for k in range(KR):
                            nc.tensor.matmul(to, thid[:, c % 3, k, h * P:(h + 1) * P],
                                             w2[:, bass.ds(e * KR + k, 1), :], start=(k == 0), stop=False)
                        ins = nc.tensor.matmul(to, ones[0:3, :], b2s[:, bass.ds(e * C, C)], start=False, stop=True)
                    ins.then_inc(typ_done, 1)

                def expert(i, c):
                    return pe.value_load(tileE[0:1, bass.ds(3 * i + c, 1)], min_val=0, max_val=E - 1)

                def body(i, c, first, last):
                    if first and c == 0:
                        turnx(i, c)
                    e = expert(i, c)
                    up(i, c, 0, e, first)
                    if not (first and c == 0):
                        down(i, c - 1, expert(i, c - 1))
                    up(i, c, 1, e, first)
                    if not last:
                        turnx(i, c + 1)
                    up(i, c, 2, e, first)
                    if last:
                        down(i, c, e)
                tiles(pe, body)

            @block.scalar
            def _(act):
                def outx(i, c, first):
                    t = 3 * i + c
                    act.wait_ge(txp_done, t + 1)
                    if not (first and c < 3):
                        act.wait_ge(ta_done, 3 * (t - 3) + 3)
                    nc.scalar.activation(txT[:, c % 3, :, :], p_tx[:, 0, 0:2 * S].rearrange("p (l n) -> p l n", l=2),
                                         ACT.Copy).then_inc(tx_done, 1)

                def body(i, c, first, last):
                    t = 3 * i + c
                    if first and c == 0:
                        outx(i, c, first)
                    e = act.value_load(tileE[0:1, bass.ds(t, 1)], min_val=0, max_val=E - 1)
                    for k in range(KR):
                        act.wait_ge(tg_done, 3 * t + k + 1)
                        if not (first and c == 0):
                            act.wait_ge(thid_done, 3 * (t - 1) + k + 1)
                        alone(act)
                        nc.scalar.activation(tgl[:, k, :], p_tg[k][:, 0:S], ACT.Gelu, scale=DOWN,
                                             bias=vcol[:, bass.ds(e * (2 * KR) + KR + k, 1)]).then_inc(tgl_done, 1)
                        if k == 1 and not last:
                            outx(i, c + 1, first)
                tiles(act, body)

            @block.vector
            def _(dve):
                def outy(i, c, first):
                    t = 3 * i + c
                    dve.wait_ge(typ_done, t + 1)
                    if not (first and c < 3):
                        dve.wait_ge(t_out[c % 3], 32 * (i + c // 3))
                    for h in range(2):
                        ins = nc.vector.tensor_scalar(tyo[:, c % 3, h, :], p_ty[:, h * P:(h + 1) * P],
                                                      tin[:, c % 3, h, P:P + 1], None, ALU.mult)
                    ins.then_inc(ty_done, 1)

                def body(i, c, first, last):
                    t = 3 * i + c
                    e = dve.value_load(tileE[0:1, bass.ds(t, 1)], min_val=0, max_val=E - 1)
                    for k in range(KR):
                        dve.wait_ge(ta_done, 3 * t + k + 1)
                        dve.wait_ge(tgl_done, 3 * t + k + 1)
                        if not first:
                            dve.wait_ge(typ_done, t - 2)
                        nc.vector.scalar_tensor_tensor(thid[:, c, k, :], p_ta[k][:, 0:S],
                                                       vup[:, bass.ds(e * (2 * KR) + k, 1)], tgl[:, k, :],
                                                       ALU.add, ALU.mult).then_inc(thid_done, 1)
                        if k == 0 and not (first and c == 0):
                            outy(i, c - 1, first)
                    if last:
                        outy(i, c, first)
                tiles(dve, body)

            @block.gpsimd
            def _(pool):
                def body(i, c, first, last):
                    pool.wait_ge(ty_done, 3 * i + c + 1)
                    alone(pool)
                    for h in range(2):
                        pool.indirect_dma_start(
                            out=y_d, out_offset=bass.IndirectOffsetOnAxis(ap=tin[:, c, h, P + 1:P + 2].bitcast(U32), axis=0),
                            in_=tyo[:, c, h, :], in_offset=None, bounds_check=2 * N - 1, oob_is_err=False
                        ).then_inc(t_out[c], 16)
                tiles(pool, body)
                for c in range(3):
                    pool.wait_ge(t_out[c], 32 * (NT // 3))

        with nc.Block() as block:
            @block.sync
            def _(sp):
                def load(i, c):
                    g = grp(i, c)
                    if not (isinstance(i, int) and g < 2):
                        sp.wait_ge(sum_done, g - 1)
                    sp.dma_start(ybuf[:, c % 2, :, :, :].rearrange("p j k c -> p j (k c)"),
                                 yg_d[g, :, :, :]).then_inc(y_in[c % 2], 16)

                def store(i, c):
                    g = grp(i, c)
                    sp.wait_ge(sum_done, g + 1)
                    sp.dma_start(og_d[g, :, :, :], acc[:, bass.ds(g * J, J), :]).then_inc(out_done, 16)
                load(0, 0)
                load(0, 1)
                with sp.Fori(1, NG // 2) as i:
                    for c in range(2):
                        load(i, c)
                        store(i, c - 2)
                store(NG // 2 - 1, 0)
                store(NG // 2 - 1, 1)
                sp.wait_ge(out_done, 16 * NG)

            @block.vector
            def _(dve):
                with dve.Fori(0, NG // 2) as i:
                    for c in range(2):
                        g = grp(i, c)
                        at = acc[:, bass.ds(g * J, J), :]
                        dve.wait_ge(y_in[c], 16 * (i + 1))
                        nc.vector.tensor_tensor(at, at, ybuf[:, c, :, 0, :], ALU.add).then_inc(add1, 1)
                        dve.wait_ge(add1, g + 1)
                        nc.vector.tensor_tensor(at, at, ybuf[:, c, :, 1, :], ALU.add).then_inc(sum_done, 1)


_INS = ['x', 'ctx_1024', 'L0_xattn_w', 'L0_xattn_u', 'L0_ffn_Ws1', 'L0_ffn_bs1', 'L0_ffn_Ws2', 'L0_ffn_bs2',
        'L0_ffn_We1', 'L0_ffn_be1', 'L0_ffn_We2', 'L0_ffn_be2', 'L0_ffn_Wr', 'L0_ffn_br']


def kernel(**inputs):
    import numpy as _np
    import concourse.bacc as _bacc
    from concourse import mybir as _mybir
    from concourse.bass_utils import run_bass_kernel_spmd as _run

    nc = _bacc.Bacc("TRN2", target_bir_lowering=False, num_devices=1)
    arrays, args = {}, []
    for name in _INS:
        a = _np.ascontiguousarray(inputs[name])
        arrays[f"in_{name}_dram"] = a
        args.append(nc.dram_tensor(f"in_{name}_dram", a.shape, _mybir.dt.from_np(a.dtype), kind="ExternalInput").ap())
    shape = inputs['x'].shape
    args.append(nc.dram_tensor("out_0_dram", shape, _mybir.dt.float32, kind="ExternalOutput").ap())
    xattn_ffn_kernel(nc, *args)
    r = _run(nc, [arrays], core_ids=[0])
    return r.results[0]["out_0_dram"]
```

```python
from contextlib import ExitStack

import concourse.bass as bass
from concourse import mybir

ALU = mybir.AluOpType
ACT = mybir.ActivationFunctionType
AX = mybir.AxisListType
F32 = mybir.dt.float32
F16 = mybir.dt.float16
BF16 = mybir.dt.bfloat16
I32 = mybir.dt.int32
U32 = mybir.dt.uint32
PE = mybir.EngineType.PE

P = 128
EPS = 1e-5
TAU = 1.5
UP = 256.0
DOWN = 1.0 / UP


def xattn_ffn_kernel(nc, x, ctx_in, w, u, Ws1, bs1, Ws2, bs2, We1, be1, We2, be2, Wr, br, out):
    BATCH, T_LEN, C = x.shape
    E = Wr.shape[1]
    N = BATCH * T_LEN
    G = 1024
    J = G // P
    H = G // 2
    JH = H // P
    NG = N // G
    HS = Ws2.shape[0]
    HR = We2.shape[1]
    KS, KR = HS // P, HR // P
    S = 256
    NT = 2 * N // S + E - 1
    CAP = N + S
    ROW = P + 2
    W = 5
    PADROW = E * CAP
    NOWHERE = 1 << 20
    assert C == P and KR == 3 and KS == 2 and NG % 2 == 0 and E == 12 and H % T_LEN == 0

    xg_d = x.rearrange("b t c -> (b t) c").rearrange("(g j p) c -> g p j c", j=J, p=P)
    cg_d = ctx_in.rearrange("b t c -> (b t) c").rearrange("(g j p) c -> g p j c", j=J, p=P)
    og_d = out.rearrange("b t c -> (b t) c").rearrange("(g j p) c -> g p j c", j=J, p=P)
    sorted_d = nc.dram_tensor("sorted_rows", (E * CAP + S, ROW), F32, kind="Internal").ap()
    y_d = nc.dram_tensor("expert_out", (2 * N, P), F32, kind="Internal").ap()
    yg_d = y_d.rearrange("(g j p k) c -> g p j (k c)", j=J, p=P, k=2)

    with ExitStack() as ctx:
        def sb(name, shape, dt):
            return ctx.enter_context(nc.sbuf_tensor(name, shape, dt))

        def ps(name, shape, dt):
            return ctx.enter_context(nc.psum_tensor(name, shape, dt))

        def sem(name):
            return ctx.enter_context(nc.semaphore(name))

        acc = sb("acc", [P, NG * J, C], F32)
        w1h = sb("w1h", [P, E * 2 * HR], F16)
        w1l = sb("w1l", [P, E * 2 * HR], F16)
        w2 = sb("w2", [P, E * KR, C], F32)
        s1f = sb("s1f", [P, 2 * HS], F32)
        s1h = sb("s1h", [P, 2 * HS], F16)
        s1l = sb("s1l", [P, 2 * HS], F16)
        s2 = sb("s2", [P, KS, C], F32)
        wrf = sb("wrf", [P, E], F32)
        wrh = sb("wrh", [P, E], F16)
        wrl = sb("wrl", [P, E], F16)
        brb = sb("brb", [P, E], F32)
        NB = E * 2 * KR + 2 * KS + 2
        WROW, UROW = NB - 2, NB - 1
        vrow = sb("vrow", [NB, P], F32)
        vcol = sb("vcol", [P, NB], F32)
        vup = sb("vup", [P, NB], F32)
        b2s = sb("b2s", [3, (E + 1) * C], BF16)
        ewu = sb("ewu", [P, 2], F32)
        decay = sb("decay", [P, 2 * H + 1], F32)
        identf = sb("identf", [P, P], F32)
        identh = sb("identh", [P, P], F16)
        diagu = sb("diagu", [P, P], F32)
        before = sb("before", [P, P], BF16)
        ones = sb("ones", [P, P], BF16)
        epsc = sb("epsc", [P, 1], F32)
        sign = sb("sign", [P, 2 * J], F32)
        eidx = sb("eidx", [P, E], F32)
        ebase = sb("ebase", [P, E], F32)
        hist = sb("hist", [P, E], BF16)
        dest = sb("dest", [P, J, 2], F32)
        pad = sb("pad", [P, 2, ROW], F32)
        counts = sb("counts", [P, E], F32)
        tab = sb("tab", [1, 8, E], F32)
        tabi = sb("tabi", [1, 2, E], I32)
        tilev = sb("tilev", [1, 8, NT], F32)
        tileno = sb("tileno", [1, NT], F32)
        tileE = sb("tileE", [1, NT], I32)
        tileR = sb("tileR", [1, NT], I32)
        padat = sb("padat", [1, E], I32)

        ct = sb("ct", [P, 2, J, C], F32)
        ek = sb("ek", [P, 2, 2, 2, H], F32)
        fw = sb("fw", [P, 2, 2 * H + 1], F32)
        bw = sb("bw", [P, 2, 2 * H + 1], F32)
        nsig = sb("nsig", [P, 2, J, C], F32)
        dens = sb("dens", [P, H], F32)
        rcp = sb("rcp", [P, H], F32)
        lnl = sb("lnl", [P, 2 * J], F32)
        bns = sb("bns", [P, 2 * J, 6], F32)
        mv = sb("mv", [P, 2 * J, 2], F32)
        lnv = sb("lnv", [P, 2 * J], F32)
        lnr = sb("lnr", [P, 2 * J], F32)
        lnm = sb("lnm", [P, 2 * J], F32)
        lng = sb("lng", [P, 2 * J], F32)
        lnscale = sb("lnscale", [P, 2 * J], F32)
        lnbias = sb("lnbias", [P, 2 * J], F32)
        xn = sb("xn", [P, J, C], F32)
        rows = sb("rows", [P, 2, J, 2, ROW], F32)
        xT = sb("xT", [P, 2, 2, H], F16)
        gl = sb("gl", [P, H], F32)
        hid = sb("hid", [P, 2, KS, H], F32)
        wst = sb("wst", [P, 2, 2 * HR], F32)
        lg = sb("lg", [P, J, E], F32)
        top = sb("top", [P, J, 8], F32)
        topi = sb("topi", [P, J, 8], U32)
        oneh = sb("oneh", [P, J, 2, E], F32)
        both = sb("both", [P, J, E], BF16)
        seen = sb("seen", [P, E], F32)
        diff = sb("diff", [P, J], F32)
        tdiff = sb("tdiff", [P, J], F32)
        place = sb("place", [P, J, E], F32)
        placed = sb("placed", [P, J, 2, E], F32)
        slot = sb("slot", [P, 2, J, 2], U32)

        b2w = (E + 1) * C
        b2f = hid[:, :, :, :].rearrange("p a k n -> p (a k n)")[0:1, 0:b2w]
        b2r = nsig[:, :, :, :].rearrange("p a j c -> p (a j c)")[0:1, 0:b2w]
        b2t = rows[:, :, :, :, :].rearrange("p a j m r -> p (a j m r)")[0:1, 0:b2w].bitcast(BF16)
        b2t = b2t.rearrange("p (a n) -> p a n", a=2)
        tile3 = bw[:, :, :].rearrange("p a n -> p (a n)")[0:1, 0:NT * E].rearrange("p (t e) -> p t e", e=E)
        tile3b = bw[:, :, :].rearrange("p a n -> p (a n)")[0:1, 1024:1024 + NT * E].rearrange("p (t e) -> p t e", e=E)
        assert NT * E <= 1024 and b2w <= 2048

        ctw = ct[:, :, :, :].rearrange("p a j c -> p (a j c)")
        tin = ctw[:, 0:W * 2 * ROW].rearrange("p (s h r) -> p s h r", s=W, h=2)
        hidw = hid[:, :, :, :].rearrange("p a k n -> p (a k n)")
        txT = hidw[:, 0:W * S].bitcast(F16).rearrange("p (s l n) -> p s l n", s=W, l=2)
        fww = fw[:, :, :].rearrange("p a n -> p (a n)")
        tgl = fww[:, 0:KR * S].rearrange("p (k n) -> p k n", k=KR)
        nsigw = nsig[:, :, :, :].rearrange("p a j c -> p (a j c)")
        tyo = nsigw[:, 0:W * S].rearrange("p (s h c) -> p s h c", s=W, h=2)
        ekw = ek[:, :, :, :, :].rearrange("p a h v n -> p (a h v n)")
        thid = ekw[:, 0:W * KR * S].rearrange("p (s k n) -> p s k n", s=W, k=KR)
        ybuf = ekw.rearrange("p (s j k c) -> p s j k c", s=2, j=J, k=2)

        p_ct = ps("p_ct", [P, H], F32)
        p_num = ps("p_num", [P, H], F32)
        p_den = ps("p_den", [P, H], F32)
        p_xT = ps("p_xT", [P, 2, H], F16)
        p_rt = ps("p_rt", [P, 512], F32)
        p_g = ps("p_g", [P, H], F32)
        p_a = ps("p_a", [P, H], F32)
        p_y = ps("p_y", [P, H], F32)
        p_lg = p_rt[:, 0:J * E]
        p_pf = p_rt[:, 128:128 + J * E]
        p_cnt = p_rt[:, 256:256 + E]
        p_vec = p_rt[:, 384:384 + NB]
        p_tg = [p_ct, p_num, p_den]
        p_ta = [p_g, p_a, p_rt]
        p_tx = p_xT
        p_ty = p_y

        passed = sem("passed")
        x_in = [sem(f"x_in{k}") for k in range(2)]
        ctx_ld = [sem(f"ctx_ld{k}") for k in range(2)]
        w_ld = [sem(f"w_ld{k}") for k in range(2)]
        sw_in = sem("sw_in")
        w2_in = sem("w2_in")
        parts_in = sem("parts_in")
        pad_out = sem("pad_out")
        scat = [sem(f"scat{k}") for k in range(2)]
        pool_const = sem("pool_const")
        dve_const = sem("dve_const")
        act_const = sem("act_const")
        pe_const = sem("pe_const")
        ctxT_done = sem("ctxT_done")
        ek_done = sem("ek_done")
        ekv_done = sem("ekv_done")
        scan_done = sem("scan_done")
        swept = sem("swept")
        nd_done = sem("nd_done")
        den_done = sem("den_done")
        rden_done = sem("rden_done")
        newton = sem("newton")
        quo_done = sem("quo_done")
        x2_done = sem("x2_done")
        bn_done = sem("bn_done")
        mv_done = sem("mv_done")
        ln_step = sem("ln_step")
        guess_done = sem("guess_done")
        lnl_done = sem("lnl_done")
        dln_done = sem("dln_done")
        nsig_done = sem("nsig_done")
        xn_done = sem("xn_done")
        hi_done = sem("hi_done")
        lo_done = sem("lo_done")
        rows_done = sem("rows_done")
        xTp_done = sem("xTp_done")
        xT_done = sem("xT_done")
        lgp_done = sem("lgp_done")
        rt_step = sem("rt_step")
        both_done = sem("both_done")
        pf_done = sem("pf_done")
        diff_done = sem("diff_done")
        tdiff_done = sem("tdiff_done")
        meta_done = sem("meta_done")
        slot_done = sem("slot_done")
        upg_done = sem("upg_done")
        upa_done = sem("upa_done")
        gl_done = sem("gl_done")
        hid_done = sem("hid_done")
        yp_done = sem("yp_done")
        acc_done = sem("acc_done")
        whi_done = sem("whi_done")
        wlo_done = sem("wlo_done")
        cnt_done = sem("cnt_done")
        tab_step = sem("tab_step")
        tab_done = sem("tab_done")
        padded = sem("padded")
        t_in = [sem(f"t_in{k}") for k in range(W)]
        t_out = [sem(f"t_out{k}") for k in range(W)]
        txp_done = sem("txp_done")
        tx_done = sem("tx_done")
        tg_done = sem("tg_done")
        ta_done = sem("ta_done")
        tgl_done = sem("tgl_done")
        thid_done = sem("thid_done")
        typ_done = sem("typ_done")
        ty_done = sem("ty_done")
        y_in = [sem(f"y_in{k}") for k in range(2)]
        add1 = sem("add1")
        sum_done = sem("sum_done")
        out_done = sem("out_done")

        SW_LOADS, POOL_CONSTS, DVE_CONSTS, META, TABS = 16 * 10, 20, 11, 3, 4
        LNS = 8

        def grp(i, c):
            return 2 * i + c

        def turn(i, c):
            return i + c // 2 + 1

        def steps(eng, body):
            for i in range(2):
                body(i, 0)
                body(i, 1)
            with eng.Fori(2, NG // 2) as i:
                body(i, 0)
                body(i, 1)
            body(NG // 2, 0)
            body(NG // 2, 1)

        def stages(i, c):
            if isinstance(i, int):
                s = grp(i, c)
                return s < NG, 1 <= s <= NG, 2 <= s <= NG + 1
            return True, True, True

        def ifat(eng, i, c, back, sm, value):
            if not isinstance(i, int) or grp(i, c) >= back:
                eng.wait_ge(sm, value)

        def alone(eng):
            eng.sem_inc(passed, 1)

        with nc.Block() as block:
            @block.sync
            def _(sp):
                def loads(i, c):
                    if not stages(i, c)[0]:
                        return
                    k, g = c % 2, grp(i, c)
                    ifat(sp, i, c, 2, ctxT_done, 2 * (g - 2) + 2)
                    sp.dma_start(ct[:, k, :, :], cg_d[g, :, :, :]).then_inc(ctx_ld[k], 16)
                    sp.dma_start(acc[:, bass.ds(g * J, J), :], xg_d[g, :, :, :]).then_inc(x_in[k], 16)

                def weights(i, c):
                    if not (stages(i, c)[0] and stages(i, c)[2]):
                        return
                    for k in range(2):
                        e = 2 * (grp(i, c) - 2) + k
                        ifat(sp, i, c, 3, wlo_done, e - 1)
                        sp.dma_start(wst[:, k, :], We1[e, :, :]).then_inc(w_ld[k], 16)

                sp.dma_start(vrow[0:E * 2 * KR, :], be1.rearrange("e (k p) -> (e k) p", p=P)).then_inc(sw_in, 16)
                sp.dma_start(vrow[E * 2 * KR:WROW, :], bs1.rearrange("(k p) -> k p", p=P)).then_inc(sw_in, 16)
                sp.dma_start(vrow[WROW:UROW, :], w[0, :, :]).then_inc(sw_in, 16)
                sp.dma_start(vrow[UROW:NB, :], u[0, :, :]).then_inc(sw_in, 16)
                sp.dma_start(b2f[:, 0:E * C], be2.rearrange("(a e) c -> a (e c)", a=1)).then_inc(sw_in, 16)
                sp.dma_start(b2f[:, E * C:], bs2.rearrange("(a c) -> a c", a=1)).then_inc(sw_in, 16)
                sp.dma_start(brb[:, :], br.partition_broadcast(P)).then_inc(sw_in, 16)
                sp.dma_start(wrf[:, :], Wr).then_inc(sw_in, 16)
                sp.dma_start(s1f[:, :], Ws1).then_inc(sw_in, 16)
                sp.dma_start(s2[:, :, :], Ws2.rearrange("(k p) d -> p k d", p=P)).then_inc(sw_in, 16)

                def body(i, c):
                    loads(i, c)
                    if isinstance(i, int) and grp(i, c) == 0:
                        sp.wait_ge(dve_const, DVE_CONSTS)
                        for m in range(2):
                            sp.dma_start(b2s[m + 1:m + 2, :], b2t[:, m, :]).then_inc(parts_in, 16)
                    weights(i, c)
                    if isinstance(i, int) and grp(i, c) == 1:
                        sp.dma_start(w2[:, :, :], We2.rearrange("e (k p) d -> p (e k) d", p=P)).then_inc(w2_in, 16)
                        sp.wait_ge(pool_const, POOL_CONSTS)
                        sp.dma_start(sorted_d[PADROW:PADROW + S, :].rearrange("(h p) r -> p h r", p=P),
                                     pad[:, :, :]).then_inc(pad_out, 16)
                steps(sp, body)
                sp.wait_ge(tab_done, 1)
                for e in range(E):
                    at = sp.value_load(padat[0:1, e:e + 1], min_val=e * CAP, max_val=e * CAP + N)
                    sp.dma_start(sorted_d[bass.ds(at, S), :].rearrange("(h p) r -> p h r", p=P),
                                 pad[:, :, :]).then_inc(padded, 16)
                sp.wait_ge(pad_out, 16)
                sp.wait_ge(padded, 16 * E)
                sp.wait_ge(w2_in, 16)
                for k in range(2):
                    sp.wait_ge(scat[k], 16 * 2 * J * (NG // 2))

            @block.gpsimd
            def _(pool):
                n = [0]

                def const(ins):
                    n[0] += 1
                    ins.then_inc(pool_const, 1)

                def behind(ins):
                    pool.wait_ge(pool_const, n[0])
                    const(ins())

                const(nc.gpsimd.memset(identf[:, :], 0.0))
                behind(lambda: nc.gpsimd.affine_select(out=identf[:, :], in_=identf[:, :], compare_op=ALU.not_equal,
                                                       fill=1.0, base=0, pattern=[[-1, P]], channel_multiplier=1))
                const(nc.gpsimd.memset(identh[:, :], 0.0))
                behind(lambda: nc.gpsimd.affine_select(out=identh[:, :], in_=identh[:, :], compare_op=ALU.not_equal,
                                                       fill=1.0, base=0, pattern=[[-1, P]], channel_multiplier=1))
                const(nc.gpsimd.memset(ones[:, :], 1.0))
                const(nc.gpsimd.memset(before[:, :], 1.0))
                behind(lambda: nc.gpsimd.affine_select(out=before[:, :], in_=before[:, :], compare_op=ALU.is_ge,
                                                       fill=0.0, base=-1, pattern=[[1, P]], channel_multiplier=-1))
                const(nc.gpsimd.memset(epsc[:, :], EPS))
                const(nc.gpsimd.memset(sign[:, 0:J], -1.0))
                const(nc.gpsimd.memset(sign[:, J:2 * J], 1.0))
                const(nc.gpsimd.memset(hist[:, :], 0.0))
                const(nc.gpsimd.iota(eidx[:, :], pattern=[[1, E]], base=0, channel_multiplier=0,
                                     allow_small_or_imprecise_dtypes=True))
                const(nc.gpsimd.iota(ebase[:, :], pattern=[[CAP, E]], base=0, channel_multiplier=0,
                                     allow_small_or_imprecise_dtypes=True))
                const(nc.gpsimd.iota(dest[:, :, :], pattern=[[2 * P, J], [1, 2]], base=0, channel_multiplier=2,
                                     allow_small_or_imprecise_dtypes=True))
                const(nc.gpsimd.iota(tileno[:, :], pattern=[[1, NT]], base=0, channel_multiplier=0,
                                     allow_small_or_imprecise_dtypes=True))
                const(nc.gpsimd.memset(pad[:, :, :], 0.0))
                behind(lambda: nc.gpsimd.memset(pad[:, :, P + 1:P + 2].bitcast(I32), NOWHERE))
                for h in range(2):
                    const(nc.gpsimd.memset(fw[:, h, 0:1], 0.0))
                const(nc.gpsimd.memset(bw[:, :, 2 * H:2 * H + 1], 0.0))
                assert n[0] == POOL_CONSTS

                def body(i, c):
                    begin, end, ffn = stages(i, c)
                    if begin or end:
                        s = grp(i, c)
                        lo, hi = (0 if begin else J), (2 * J if end else J)

                        def small(n, out, in0, in1, op=ALU.mult):
                            if not (isinstance(s, int) and s == 0 and n == 0):
                                pool.wait_ge(ln_step, LNS * s + n)
                                alone(pool)
                            if isinstance(in1, tuple):
                                ins = nc.gpsimd.tensor_scalar(out, in0, in1[0], in1[1], *in1[2:])
                            else:
                                ins = nc.gpsimd.tensor_tensor(out, in0, in1, op)
                            ins.then_inc(ln_step, 1)
                        pool.wait_ge(mv_done, s + 1)
                        alone(pool)
                        small(0, lnv[:, lo:hi], mv[:, lo:hi, 1], (EPS, None, ALU.add))
                        small(1, lnm[:, lo:hi], mv[:, lo:hi, 0], (-1.0, None, ALU.mult))
                        pool.wait_ge(guess_done, s + 1)
                        alone(pool)
                        small(2, lnr[:, lo:hi], lng[:, lo:hi], lng[:, lo:hi])
                        small(3, lnr[:, lo:hi], lnr[:, lo:hi], lnv[:, lo:hi])
                        small(4, lnr[:, lo:hi], lnr[:, lo:hi], (-0.5, 1.5, ALU.mult, ALU.add))
                        small(5, lnr[:, lo:hi], lnr[:, lo:hi], lng[:, lo:hi])
                        if not isinstance(i, int) or s >= 1:
                            pool.wait_ge(nsig_done, s if not isinstance(i, int) else min(s, NG))
                            alone(pool)
                        if not isinstance(i, int) or s >= 2:
                            pool.wait_ge(xn_done, s - 1)
                            alone(pool)
                        small(6, lnscale[:, lo:hi], lnr[:, lo:hi], sign[:, lo:hi])
                        small(7, lnbias[:, lo:hi], lnscale[:, lo:hi], lnm[:, lo:hi])
                    if end:
                        k, g = (c - 1) % 2, grp(i, c - 1)
                        pool.wait_ge(hi_done, g + 1)
                        alone(pool)
                        nc.gpsimd.tensor_tensor(rows[:, k, :, 0, C // 2:C].bitcast(F16), xn[:, :, :],
                                                rows[:, k, :, 0, 0:C // 2].bitcast(F16), ALU.subtract).then_inc(lo_done, 1)
                    if ffn:
                        k, g = (c - 2) % 2, grp(i, c - 2)
                        pool.wait_ge(slot_done, g + 1)
                        alone(pool)
                        pool.wait_ge(meta_done, META * (g + 1))
                        alone(pool)
                        pool.wait_ge(rows_done, g + 1)
                        alone(pool)
                        for j in range(J):
                            for m in range(2):
                                pool.indirect_dma_start(
                                    out=sorted_d, out_offset=bass.IndirectOffsetOnAxis(ap=slot[:, k, j, m:m + 1], axis=0),
                                    in_=rows[:, k, j, m, :], in_offset=None).then_inc(scat[k], 16)
                steps(pool, body)

            @block.scalar
            def _(act):
                nc.scalar.preload_act_table_set("natural_log_exp_and_others")
                act.wait_ge(sw_in, SW_LOADS)
                nc.scalar.activation(s1h[:, :], s1f[:, :], ACT.Copy, scale=UP).then_inc(act_const, 1)
                nc.scalar.activation(wrh[:, :], wrf[:, :], ACT.Copy, scale=UP).then_inc(act_const, 1)
                act.wait_ge(pe_const, 1)
                nc.scalar.activation(vcol[:, :], p_vec, ACT.Copy).then_inc(act_const, 1)
                act.wait_ge(act_const, 3)
                nc.scalar.activation(ewu[:, :], vcol[:, WROW:NB], ACT.Exp).then_inc(act_const, 1)

                def exps(i, c, h):
                    g = grp(i, c)
                    act.wait_ge(ctxT_done, 2 * g + h + 1)
                    ifat(act, i, c, 2, nd_done, 2 * (g - 2) + h + 1)
                    nc.scalar.activation(ek[:, c % 2, h, 1, :], p_ct[:, :], ACT.Exp).then_inc(ek_done, 1)

                def reciprocal(i, c, h):
                    n = 2 * grp(i, c) + h
                    act.wait_ge(den_done, n + 1)
                    if not (isinstance(i, int) and n == 0):
                        act.wait_ge(x2_done, n)
                    nc.scalar.activation(rcp[:, :], dens[:, :], ACT.Ln).then_inc(dln_done, 1)
                    act.wait_ge(dln_done, n + 1)
                    nc.scalar.activation(rcp[:, :], rcp[:, :], ACT.Exp, scale=-1.0).then_inc(rden_done, 1)

                def outx(i, c, h):
                    g = grp(i, c)
                    act.wait_ge(xTp_done, 2 * g + h + 1)
                    ifat(act, i, c, 1, upa_done, 4 * (g - 1) + 2 * h + 2)
                    ifat(act, i, c, 1, lgp_done, g)
                    nc.scalar.activation(xT[:, h, :, :], p_xT[:, :, :], ACT.Copy).then_inc(xT_done, 1)

                def gelu(i, c, h, f):
                    n = 4 * grp(i, c) + 2 * h + f
                    act.wait_ge(upg_done, n + 1)
                    if not (isinstance(i, int) and n == 0):
                        act.wait_ge(hid_done, n)
                    nc.scalar.activation(gl[:, :], p_g[:, :], ACT.Gelu, scale=DOWN,
                                         bias=vcol[:, E * 2 * KR + KS + f:E * 2 * KR + KS + f + 1]).then_inc(gl_done, 1)

                def weigh(i, c):
                    g = grp(i, c)
                    act.wait_ge(diff_done, g + 1)
                    ifat(act, i, c, 1, meta_done, META * g)
                    nc.scalar.activation(tdiff[:, :], diff[:, :], ACT.Tanh, scale=0.5 / TAU).then_inc(tdiff_done, 1)

                def guess(i, c, lo, hi):
                    s = grp(i, c)
                    act.wait_ge(mv_done, s + 1)
                    ifat(act, i, c, 1, ln_step, LNS * s)
                    nc.scalar.activation(lnl[:, lo:hi], mv[:, lo:hi, 1], ACT.Ln, bias=epsc[:, 0:1]).then_inc(lnl_done, 1)
                    act.wait_ge(lnl_done, s + 1)
                    nc.scalar.activation(lng[:, lo:hi], lnl[:, lo:hi], ACT.Exp, scale=-0.5).then_inc(guess_done, 1)

                def weights(i, c):
                    for k in range(2):
                        e = 2 * grp(i, c) + k
                        act.wait_ge(w_ld[k], 16 * (grp(i, c) + 1))
                        alone(act)
                        nc.scalar.activation(w1h[:, bass.ds(e * 2 * HR, 2 * HR)], wst[:, k, :], ACT.Copy,
                                             scale=UP).then_inc(whi_done, 1)

                def sigmoids(i, c):
                    k, g = c % 2, grp(i, c)
                    ifat(act, i, c, 2, den_done, 2 * (g - 2) + 2)
                    alone(act)
                    for j in range(J):
                        ins = nc.scalar.activation(nsig[:, k, j, :], acc[:, g * J + j, :], ACT.Exp,
                                                   scale=lnscale[:, j:j + 1], bias=lnbias[:, j:j + 1])
                    ins.then_inc(nsig_done, 1)

                def normed(i, c):
                    k, g = c % 2, grp(i, c)
                    ifat(act, i, c, 1, lo_done, g)
                    alone(act)
                    for j in range(J):
                        ins = nc.scalar.activation(xn[:, j, :], acc[:, g * J + j, :], ACT.Identity,
                                                   scale=lnscale[:, J + j:J + j + 1], bias=lnbias[:, J + j:J + j + 1])
                    ins.then_inc(xn_done, 1)
                    act.wait_ge(xn_done, g + 1)
                    ifat(act, i, c, 2, xTp_done, 2 * (g - 2) + 2)
                    ifat(act, i, c, 2, scat[k], 16 * 2 * J * (turn(i, c) - 1))
                    alone(act)
                    nc.scalar.activation(rows[:, k, :, 0, 0:C // 2].bitcast(F16), xn[:, :, :],
                                         ACT.Copy).then_inc(hi_done, 1)

                def body(i, c):
                    begin, end, ffn = stages(i, c)
                    if end:
                        reciprocal(i, c - 1, 0)
                    if ffn:
                        outx(i, c - 2, 0)
                    if begin:
                        exps(i, c, 0)
                    if ffn:
                        outx(i, c - 2, 1)
                    if begin:
                        exps(i, c, 1)
                    if end:
                        reciprocal(i, c - 1, 1)
                    if begin or end:
                        guess(i, c, 0 if begin else J, 2 * J if end else J)
                    if begin and ffn:
                        weights(i, c - 2)
                    if begin or end:
                        act.wait_ge(ln_step, LNS * grp(i, c) + LNS)
                        alone(act)
                    if begin:
                        sigmoids(i, c)
                    if end:
                        normed(i, c - 1)
                    if ffn:
                        gelu(i, c - 2, 0, 0)
                        weigh(i, c - 2)
                        gelu(i, c - 2, 0, 1)
                        gelu(i, c - 2, 1, 0)
                        gelu(i, c - 2, 1, 1)
                        nc.scalar.preload_act_table_set("natural_log_exp_and_others")
                steps(act, body)

            @block.vector
            def _(dve):
                n = [0]

                def const(ins, wait=True):
                    n[0] += 1
                    ins.then_inc(dve_const, 1)
                    if wait:
                        dve.wait_ge(dve_const, n[0])

                dve.wait_ge(sw_in, SW_LOADS)
                dve.wait_ge(act_const, 4)
                dve.wait_ge(pool_const, POOL_CONSTS)
                const(nc.vector.tensor_copy(decay[:, :], ewu[:, 0:1].to_broadcast([P, 2 * H + 1])))
                const(nc.vector.memset(decay[:, 0:2 * H + 1:T_LEN], 0.0), False)
                const(nc.vector.tensor_scalar(diagu[:, :], identf[:, :], ewu[:, 1:2], None, ALU.mult), False)
                const(nc.vector.tensor_scalar(vup[:, :], vcol[:, :], UP, None, ALU.mult), False)
                const(nc.vector.scalar_tensor_tensor(s1l[:, :], s1f[:, :], UP, s1h[:, :], ALU.mult, ALU.subtract), False)
                const(nc.vector.scalar_tensor_tensor(wrl[:, :], wrf[:, :], UP, wrh[:, :], ALU.mult, ALU.subtract), False)
                const(nc.vector.tensor_scalar(b2r[:, :], b2f[:, :], UP, None, ALU.mult))
                const(nc.vector.tensor_copy(b2s[0:1, :], b2r[:, :]))
                const(nc.vector.tensor_tensor(b2f[:, :], b2r[:, :], b2s[0:1, :], ALU.subtract))
                const(nc.vector.tensor_copy(b2t[:, 0, :], b2f[:, :]))
                const(nc.vector.tensor_tensor(b2t[:, 1, :], b2f[:, :], b2t[:, 0, :], ALU.subtract))
                dve.wait_ge(parts_in, 32)
                assert n[0] == DVE_CONSTS

                def ekv(i, c, h):
                    g = grp(i, c)
                    dve.wait_ge(ek_done, 2 * g + h + 1)
                    nc.vector.tensor_tensor(ek[:, c % 2, h, 0, :], ek[:, c % 2, h, 1, :], p_ct[:, :],
                                            ALU.mult).then_inc(ekv_done, 1)

                def scan(i, c, h):
                    g = grp(i, c)
                    dve.wait_ge(ekv_done, 2 * g + h + 1)
                    ifat(dve, i, c, 1, nd_done, 2 * (g - 1) + h + 1)
                    src = ek[:, c % 2, h, :, :].rearrange("p v n -> p (v n)")
                    nc.vector.tensor_tensor_scan(fw[:, h, 1:2 * H + 1], decay[:, 0:2 * H], src, 0.0,
                                                 ALU.mult, ALU.add).then_inc(swept, 1)
                    nc.vector.tensor_tensor_scan(back(bw[:, h, 0:2 * H]), back(decay[:, 1:2 * H + 1]), back(src), 0.0,
                                                 ALU.mult, ALU.add).then_inc(swept, 1)
                    dve.wait_ge(swept, 4 * g + 2 * h + 2)
                    nc.vector.memset(fw[:, h, T_LEN:2 * H + 1:T_LEN], 0.0)
                    nc.vector.memset(bw[:, h, 0:2 * H:T_LEN], 0.0).then_inc(scan_done, 1)

                def back(a):
                    p, (_, m) = a.ap[0], a.ap[-1]
                    return bass.AP(a.tensor, a.offset + m - 1, [list(p), [-1, m]])

                def den(i, c, h):
                    k, g = c % 2, grp(i, c)
                    dve.wait_ge(nd_done, 2 * g + h + 1)
                    dve.wait_ge(nsig_done, g + 1)
                    if not (isinstance(i, int) and g == 0 and h == 0):
                        dve.wait_ge(x2_done, 2 * g + h)
                    nc.vector.scalar_tensor_tensor(dens[:, :], nsig[:, k, h * JH:(h + 1) * JH, :].rearrange("p j c -> p (j c)"),
                                                   1.0, p_den[:, :], ALU.add, ALU.mult).then_inc(den_done, 1)

                def add(i, c, h):
                    g = grp(i, c)
                    n = 2 * g + h
                    dve.wait_ge(rden_done, n + 1)
                    nc.vector.tensor_tensor(dens[:, :], dens[:, :], rcp[:, :], ALU.mult).then_inc(newton, 1)
                    nc.vector.tensor_tensor(rcp[:, :], p_num[:, :], rcp[:, :], ALU.mult).then_inc(quo_done, 1)
                    dve.wait_ge(quo_done, n + 1)
                    nc.vector.scalar_tensor_tensor(rcp[:, :], dens[:, :], 2.0, rcp[:, :], ALU.subtract, ALU.mult).then_inc(newton, 1)
                    dve.wait_ge(newton, 2 * n + 2)
                    at = acc[:, bass.ds(g * J + h * JH, JH), :].rearrange("p j c -> p (j c)")
                    nc.vector.tensor_tensor(at, at, rcp[:, :], ALU.subtract).then_inc(x2_done, 1)

                def geglu(i, c, h, f):
                    g = grp(i, c)
                    n = 4 * g + 2 * h + f
                    dve.wait_ge(upa_done, n + 1)
                    dve.wait_ge(gl_done, n + 1)
                    ifat(dve, i, c, 1, yp_done, 2 * (g - 1) + h + 1)
                    nc.vector.scalar_tensor_tensor(hid[:, h, f, :], p_a[:, :], vup[:, E * 2 * KR + f:E * 2 * KR + f + 1],
                                                   gl[:, :], ALU.add, ALU.mult).then_inc(hid_done, 1)

                def addffn(i, c, h):
                    g = grp(i, c)
                    dve.wait_ge(yp_done, 2 * g + h + 1)
                    at = acc[:, bass.ds(g * J + h * JH, JH), :].rearrange("p j c -> p (j c)")
                    nc.vector.scalar_tensor_tensor(at, p_y[:, :], DOWN, at, ALU.mult, ALU.add).then_inc(acc_done, 1)

                def route(i, c):
                    g = grp(i, c)
                    dve.wait_ge(lgp_done, g + 1)
                    ifat(dve, i, c, 1, rt_step, 5 * g)
                    ifat(dve, i, c, 1, tab_step, TABS * g)
                    ifat(dve, i, c, 1, meta_done, META * g)
                    nc.vector.scalar_tensor_tensor(lg[:, :, :], p_lg.rearrange("p (j e) -> p j e", e=E), DOWN,
                                                   brb[:, None, :].to_broadcast([P, J, E]), ALU.mult, ALU.add).then_inc(rt_step, 1)
                    dve.wait_ge(rt_step, 5 * g + 1)
                    alone(dve)
                    for j in range(J):
                        ins = nc.vector.max(top[:, j, :], lg[:, j, :])
                    ins.then_inc(rt_step, 1)
                    dve.wait_ge(rt_step, 5 * g + 2)
                    alone(dve)
                    for j in range(J):
                        ins = nc.vector.max_index(topi[:, j, :], top[:, j, :], lg[:, j, :])
                    ifat(dve, i, c, 1, tdiff_done, g)
                    nc.vector.tensor_tensor(diff[:, :], top[:, :, 0], top[:, :, 1], ALU.subtract).then_inc(diff_done, 1)
                    ins.then_inc(rt_step, 1)
                    dve.wait_ge(rt_step, 5 * g + 3)
                    nc.vector.tensor_tensor(oneh[:, :, :, :], topi[:, :, 0:2, None].to_broadcast([P, J, 2, E]),
                                            eidx[:, None, None, :].to_broadcast([P, J, 2, E]),
                                            ALU.is_equal).then_inc(rt_step, 1)
                    dve.wait_ge(rt_step, 5 * g + 4)
                    ifat(dve, i, c, 1, pf_done, g)
                    nc.vector.tensor_tensor(both[:, :, :], oneh[:, :, 0, :], oneh[:, :, 1, :], ALU.add).then_inc(both_done, 1)

                def assign(i, c):
                    k, g = c % 2, grp(i, c)
                    meta = rows[:, k, :, :, :]
                    dve.wait_ge(pf_done, g + 1)
                    nc.vector.tensor_tensor(place[:, :, :], p_pf.rearrange("p (j e) -> p j e", e=E),
                                            ebase[:, None, :].to_broadcast([P, J, E]), ALU.add).then_inc(rt_step, 1)
                    nc.vector.tensor_reduce(seen[:, :], both[:, :, :].rearrange("p j e -> p e j"), AX.X, ALU.add).then_inc(tab_step, 1)
                    ifat(dve, i, c, 2, scat[k], 16 * 2 * J * (turn(i, c) - 1))
                    nc.vector.tensor_copy(meta[:, :, :, P + 1].bitcast(I32), dest[:, :, :]).then_inc(meta_done, 1)
                    dve.wait_ge(rt_step, 5 * g + 5)
                    nc.vector.tensor_tensor(placed[:, :, :, :], oneh[:, :, :, :],
                                            place[:, :, None, :].to_broadcast([P, J, 2, E]), ALU.mult).then_inc(tab_step, 1)
                    dve.wait_ge(tab_step, TABS * g + 1)
                    nc.vector.tensor_tensor(hist[:, :], hist[:, :], seen[:, :], ALU.add).then_inc(tab_step, 1)
                    dve.wait_ge(meta_done, META * g + 1)
                    nc.vector.tensor_scalar(dest[:, :, :], dest[:, :, :], 2.0 * G, None, ALU.add).then_inc(tab_step, 1)
                    dve.wait_ge(tab_step, TABS * g + 2)
                    with nc.allow_low_precision(reason="a row's number, a whole number below 2**24"):
                        nc.vector.tensor_reduce(slot[:, k, :, :], placed[:, :, :, :], AX.X, ALU.add).then_inc(slot_done, 1)
                    dve.wait_ge(tdiff_done, g + 1)
                    nc.vector.tensor_scalar(meta[:, :, 0, P], tdiff[:, :], DOWN / 2, DOWN / 2, ALU.mult, ALU.add).then_inc(meta_done, 1)
                    nc.vector.tensor_scalar(meta[:, :, 1, P], tdiff[:, :], -DOWN / 2, DOWN / 2, ALU.mult, ALU.add).then_inc(meta_done, 1)

                def stats(i, c, at):
                    g = grp(i, c)
                    for j in range(J):
                        ins = nc.vector.bn_stats(bns[:, at + j, :], acc[:, g * J + j, :])
                    ins.then_inc(bn_done, 1)

                def aggregate(i, c, lo, hi):
                    s = grp(i, c)
                    if not isinstance(i, int):
                        dve.wait_ge(bn_done, 2 * s + 1)
                    else:
                        dve.wait_ge(bn_done, min(s + 1, NG) + min(s, NG))
                    ifat(dve, i, c, 1, ln_step, LNS * s)
                    alone(dve)
                    for j in range(lo, hi):
                        ins = nc.vector.bn_aggr(mv[:, j, :], bns[:, j, :])
                    ins.then_inc(mv_done, 1)

                def weights(i, c):
                    for k in range(2):
                        e = 2 * grp(i, c) + k
                        dve.wait_ge(whi_done, e + 1)
                        nc.vector.scalar_tensor_tensor(w1l[:, bass.ds(e * 2 * HR, 2 * HR)], wst[:, k, :], UP,
                                                       w1h[:, bass.ds(e * 2 * HR, 2 * HR)],
                                                       ALU.mult, ALU.subtract).then_inc(wlo_done, 1)

                def second(i, c):
                    k, g = c % 2, grp(i, c)
                    dve.wait_ge(lo_done, g + 1)
                    ifat(dve, i, c, 2, scat[k], 16 * 2 * J * (turn(i, c) - 1))
                    nc.vector.tensor_copy(rows[:, k, :, 1, 0:C], rows[:, k, :, 0, 0:C]).then_inc(rows_done, 1)

                def body(i, c):
                    begin, end, ffn = stages(i, c)
                    s = grp(i, c)
                    if end:
                        den(i, c - 1, 0)
                    if begin or end:
                        ifat(dve, i, c, 1, mv_done, s)
                    if begin:
                        dve.wait_ge(x_in[c % 2], 16 * turn(i, c))
                        alone(dve)
                        stats(i, c, 0)
                    if end:
                        add(i, c - 1, 0)
                    if begin:
                        ekv(i, c, 0)
                    if end:
                        den(i, c - 1, 1)
                    if begin:
                        scan(i, c, 0)
                    if end:
                        add(i, c - 1, 1)
                        dve.wait_ge(x2_done, 2 * grp(i, c - 1) + 2)
                        alone(dve)
                        stats(i, c - 1, J)
                    if begin or end:
                        aggregate(i, c, 0 if begin else J, 2 * J if end else J)
                    if ffn:
                        route(i, c - 2)
                    if begin:
                        ekv(i, c, 1)
                        scan(i, c, 1)
                    if begin and ffn:
                        weights(i, c - 2)
                    if ffn:
                        geglu(i, c - 2, 0, 0)
                        geglu(i, c - 2, 0, 1)
                        geglu(i, c - 2, 1, 0)
                        addffn(i, c - 2, 0)
                        geglu(i, c - 2, 1, 1)
                        assign(i, c - 2)
                    if end:
                        second(i, c - 1)
                    if ffn:
                        addffn(i, c - 2, 1)
                steps(dve, body)

                n = [TABS * NG]

                def link(ins):
                    n[0] += 1
                    ins.then_inc(tab_step, 1)
                    dve.wait_ge(tab_step, n[0])

                def row(k):
                    return tab[:, k, :]

                def trow(k):
                    return tilev[:, k, :]

                dve.wait_ge(cnt_done, 1)
                link(nc.vector.tensor_copy(counts[:, :], p_cnt))
                link(nc.vector.tensor_scalar(tabi[:, 0, :], counts[0:1, :], float(S - 1), None, ALU.add))
                link(nc.vector.tensor_scalar(tabi[:, 1, :], tabi[:, 0, :], S.bit_length() - 1, None,
                                             ALU.logical_shift_right))
                link(nc.vector.tensor_copy(row(0), tabi[:, 1, :]))
                link(nc.vector.memset(row(2), 1.0))
                link(nc.vector.tensor_tensor_scan(row(1), row(2), row(0), 0.0, ALU.mult, ALU.add))
                link(nc.vector.tensor_tensor(row(3), row(1), row(0), ALU.subtract))
                link(nc.vector.scalar_tensor_tensor(row(4), row(3), -float(S), ebase[0:1, :], ALU.mult, ALU.add))
                link(nc.vector.tensor_tensor(tile3[:, :, :], tileno[:, :, None].to_broadcast([1, NT, E]),
                                             tab[:, 1:2, :].to_broadcast([1, NT, E]), ALU.is_ge))
                link(nc.vector.tensor_reduce(trow(0), tile3[:, :, :], AX.X, ALU.add))
                link(nc.vector.tensor_scalar(tileE[:, :], trow(0), float(E - 1), None, ALU.min))
                link(nc.vector.tensor_tensor(tile3b[:, :, :], eidx[0:1, None, :].to_broadcast([1, NT, E]),
                                             tilev[:, 0, :, None].to_broadcast([1, NT, E]), ALU.is_equal))
                link(nc.vector.tensor_tensor(tile3[:, :, :], tile3b[:, :, :], tab[:, 4:5, :].to_broadcast([1, NT, E]),
                                             ALU.mult))
                link(nc.vector.tensor_reduce(trow(1), tile3[:, :, :], AX.X, ALU.add))
                link(nc.vector.tensor_scalar(trow(2), tileno[:, :], float(S), None, ALU.mult))
                link(nc.vector.tensor_tensor(trow(3), trow(1), trow(2), ALU.add))
                link(nc.vector.tensor_scalar(trow(4), trow(2), -1.0, float(PADROW), ALU.mult, ALU.add))
                link(nc.vector.tensor_scalar(trow(5), trow(0), float(E), None, ALU.is_ge))
                link(nc.vector.tensor_tensor(trow(6), trow(4), trow(5), ALU.mult))
                link(nc.vector.tensor_tensor(tileR[:, :], trow(3), trow(6), ALU.add))
                nc.vector.tensor_tensor(padat[:, :], counts[0:1, :], ebase[0:1, :], ALU.add).then_inc(tab_done, 1)

            @block.tensor
            def _(pe):
                pe.wait_ge(sw_in, SW_LOADS)
                pe.wait_ge(pool_const, POOL_CONSTS)
                nc.tensor.transpose(p_vec, vrow[:, :], identf[0:NB, 0:NB]).then_inc(pe_const, 1)
                pe.wait_ge(act_const, 4)
                pe.wait_ge(dve_const, DVE_CONSTS)
                pe.wait_ge(parts_in, 32)

                def ctxT(i, c, h):
                    k, g = c % 2, grp(i, c)
                    if h == 0:
                        pe.wait_ge(ctx_ld[k], 16 * turn(i, c))
                    if not (isinstance(i, int) and g == 0 and h == 0):
                        pe.wait_ge(ekv_done, 2 * g + h)
                    for j in range(JH):
                        ins = nc.tensor.transpose(p_ct[:, j * P:(j + 1) * P], ct[:, k, h * JH + j, :], identf[:, :])
                    ins.then_inc(ctxT_done, 1)

                def numden(i, c, h):
                    k, g = c % 2, grp(i, c)
                    pe.wait_ge(scan_done, 2 * g + h + 1)
                    if not (isinstance(i, int) and g == 0 and h == 0):
                        pe.wait_ge(quo_done, 2 * g + h)
                    for v, bank in ((1, p_den), (0, p_num)):
                        for j in range(JH):
                            to = bank[:, j * P:(j + 1) * P]
                            a = v * H + j * P
                            nc.tensor.matmul(to, fw[:, h, a:a + P], identf[:, :], start=True, stop=False)
                            nc.tensor.matmul(to, bw[:, h, a + 1:a + 1 + P], identf[:, :], start=False, stop=False)
                            ins = nc.tensor.matmul(to, ek[:, k, h, v, j * P:(j + 1) * P], diagu[:, :],
                                                   start=False, stop=True)
                    ins.then_inc(nd_done, 1)

                def turnx(i, c, h):
                    k, g = c % 2, grp(i, c)
                    pe.wait_ge(lo_done, g + 1)
                    if not (isinstance(i, int) and g == 0 and h == 0):
                        pe.wait_ge(xT_done, 2 * g + h)
                    for l in range(2):
                        for j in range(JH):
                            ins = nc.tensor.transpose(
                                p_xT[:, l, j * P:(j + 1) * P],
                                rows[:, k, h * JH + j, 0, l * (C // 2):(l + 1) * (C // 2)].bitcast(F16), identh[:, :])
                    ins.then_inc(xTp_done, 1)

                def router(i, c):
                    g = grp(i, c)
                    pe.wait_ge(xT_done, 2 * g + 2)
                    ifat(pe, i, c, 1, slot_done, g)
                    for j in range(J):
                        xh = xT[:, j // JH, 0, (j % JH) * P:(j % JH + 1) * P]
                        xl = xT[:, j // JH, 1, (j % JH) * P:(j % JH + 1) * P]
                        to = p_lg[:, j * E:(j + 1) * E]
                        nc.tensor.matmul(to, xh, wrh[:, :], start=True, stop=False)
                        nc.tensor.matmul(to, xh, wrl[:, :], start=False, stop=False)
                        ins = nc.tensor.matmul(to, xl, wrh[:, :], start=False, stop=True)
                    ins.then_inc(lgp_done, 1)

                def prefix(i, c):
                    g = grp(i, c)
                    pe.wait_ge(both_done, g + 1)
                    ifat(pe, i, c, 1, slot_done, g)
                    nc.tensor.matmul(p_pf, before[:, :], both[:, :, :].rearrange("p j e -> p (j e)"), start=True, stop=False)
                    for j in range(J - 1):
                        nc.tensor.matmul(p_pf[:, (j + 1) * E:J * E], ones[:, :],
                                         both[:, j:j + 1, :].to_broadcast([P, J - 1 - j, E]), start=False, stop=False)
                    nc.tensor.matmul(p_pf, ones[:, :], hist[:, None, :].to_broadcast([P, J, E]),
                                     start=False, stop=True).then_inc(pf_done, 1)

                def up(i, c, h, f):
                    g = grp(i, c)
                    n = 4 * g + 2 * h + f
                    pe.wait_ge(xT_done, 2 * g + h + 1)
                    for bank, off, done, used in ((p_g, HS, upg_done, gl_done), (p_a, 0, upa_done, hid_done)):
                        if not (isinstance(i, int) and g == 0 and h == 0 and f == 0):
                            pe.wait_ge(used, n)
                        cols = slice(off + f * P, off + (f + 1) * P)
                        nc.tensor.matmul(bank[:, :], s1h[:, cols], xT[:, h, 0, :], start=True, stop=False)
                        nc.tensor.matmul(bank[:, :], s1h[:, cols], xT[:, h, 1, :], start=False, stop=False)
                        nc.tensor.matmul(bank[:, :], s1l[:, cols], xT[:, h, 0, :], start=False, stop=True).then_inc(done, 1)

                def down(i, c, h):
                    g = grp(i, c)
                    pe.wait_ge(hid_done, 4 * g + 2 * h + 2)
                    if not (isinstance(i, int) and g == 0 and h == 0):
                        pe.wait_ge(acc_done, 2 * g + h)
                    for j in range(JH):
                        to = p_y[:, j * P:(j + 1) * P]
                        for f in range(KS):
                            nc.tensor.matmul(to, hid[:, h, f, j * P:(j + 1) * P], s2[:, f, :], start=(f == 0), stop=False)
                        ins = nc.tensor.matmul(to, ones[0:3, :], b2s[:, E * C:(E + 1) * C], start=False, stop=True)
                    ins.then_inc(yp_done, 1)

                def body(i, c):
                    begin, end, ffn = stages(i, c)
                    if end:
                        numden(i, c - 1, 0)
                    if ffn:
                        turnx(i, c - 2, 0)
                    if begin:
                        ctxT(i, c, 0)
                    if ffn:
                        turnx(i, c - 2, 1)
                    if end:
                        numden(i, c - 1, 1)
                    if begin:
                        ctxT(i, c, 1)
                    if ffn:
                        router(i, c - 2)
                        up(i, c - 2, 0, 0)
                        up(i, c - 2, 0, 1)
                        up(i, c - 2, 1, 0)
                        down(i, c - 2, 0)
                        up(i, c - 2, 1, 1)
                        prefix(i, c - 2)
                        down(i, c - 2, 1)
                steps(pe, body)
                pe.wait_ge(tab_step, TABS * NG)
                nc.tensor.matmul(p_cnt, ones[:, :], hist[:, :], start=True, stop=True).then_inc(cnt_done, 1)

        def tiles(eng, kind, table, low, high, body):
            def round_of(i, first, last):
                which = {c: v for c, v in enumerate(fetch(table[0:1, bass.ds(W * i, W)]))}
                if not first:
                    which[-1] = fetch(table[0:1, bass.ds(W * i - 1, 1)])[0] if kind == PE else None
                for c in range(W):
                    body(i, c, which, first, last)

            def fetch(values):
                return nc.values_load_multi_w_load_instructions(values, engines=[kind], min_val=low, max_val=high,
                    skip_runtime_bounds_check_because='the table is made of numbers in this range')[1]

            round_of(0, True, False)
            with eng.Fori(1, NT // W - 1) as i:
                round_of(i, False, False)
            round_of(NT // W - 1, False, True)
        assert NT % W == 0

        with nc.Block() as block:
            @block.sync
            def _(sp):
                def body(i, c, row, first, last):
                    if not first:
                        sp.wait_ge(t_out[c], 32 * i)
                    sp.dma_start(tin[:, c, :, :], sorted_d[bass.ds(row[c], S), :].rearrange("(h p) r -> p h r", p=P)
                                 ).then_inc(t_in[c], 16)
                tiles(sp, mybir.EngineType.SP, tileR, 0, PADROW, body)

            @block.tensor
            def _(pe):
                def turnx(i, c):
                    t = W * i + c
                    pe.wait_ge(t_in[c % W], 16 * (i + c // W + 1))
                    if not (isinstance(i, int) and t == 0):
                        pe.wait_ge(tx_done, t)
                    for l in range(2):
                        for h in range(2):
                            ins = nc.tensor.transpose(p_tx[:, 0, l * S + h * P:l * S + (h + 1) * P],
                                                      tin[:, c % W, h, l * (C // 2):(l + 1) * (C // 2)].bitcast(F16),
                                                      identh[:, :])
                    ins.then_inc(txp_done, 1)

                def up(i, c, k, e, first):
                    t = W * i + c
                    if k == 0:
                        pe.wait_ge(tx_done, t + 1)
                    if not (first and c == 0):
                        pe.wait_ge(thid_done, KR * (t - 1) + k + 1)
                    xh, xl = txT[:, c, 0, :], txT[:, c, 1, :]
                    for bank, off, done in ((p_tg[k], KR + k, tg_done), (p_ta[k], k, ta_done)):
                        to = bank[:, 0:S]
                        cols = bass.ds(e * (2 * HR) + off * P, P)
                        nc.tensor.matmul(to, w1h[:, cols], xh, start=True, stop=False)
                        nc.tensor.matmul(to, w1h[:, cols], xl, start=False, stop=False)
                        nc.tensor.matmul(to, w1l[:, cols], xh, start=False, stop=True).then_inc(done, 1)

                def down(i, c, e):
                    t = W * i + c
                    pe.wait_ge(thid_done, KR * t + KR)
                    if not (isinstance(i, int) and t == 0):
                        pe.wait_ge(ty_done, t)
                    for h in range(2):
                        to = p_ty[:, h * P:(h + 1) * P]
                        for k in range(KR):
                            nc.tensor.matmul(to, thid[:, c % W, k, h * P:(h + 1) * P],
                                             w2[:, bass.ds(e * KR + k, 1), :], start=(k == 0), stop=False)
                        ins = nc.tensor.matmul(to, ones[0:3, :], b2s[:, bass.ds(e * C, C)], start=False, stop=True)
                    ins.then_inc(typ_done, 1)

                def body(i, c, expert, first, last):
                    if first and c == 0:
                        turnx(i, 0)
                        turnx(i, 1)
                    e = expert[c]
                    up(i, c, 0, e, first)
                    up(i, c, 1, e, first)
                    if not (first and c == 0):
                        down(i, c - 1, expert[c - 1])
                    if not (last and c + 2 >= W):
                        turnx(i, c + 2)
                    up(i, c, 2, e, first)
                    if last and c == W - 1:
                        down(i, c, e)
                tiles(pe, PE, tileE, 0, E - 1, body)

            @block.scalar
            def _(act):
                def outx(i, c, first):
                    t = W * i + c
                    act.wait_ge(txp_done, t + 1)
                    if not (first and c < W):
                        act.wait_ge(ta_done, KR * (t - W) + KR)
                    nc.scalar.activation(txT[:, c % W, :, :], p_tx[:, 0, 0:2 * S].rearrange("p (l n) -> p l n", l=2),
                                         ACT.Copy).then_inc(tx_done, 1)

                def body(i, c, expert, first, last):
                    t, e = W * i + c, expert[c]
                    if first and c == 0:
                        outx(i, 0, first)
                        outx(i, 1, first)
                    for k in range(KR):
                        act.wait_ge(tg_done, KR * t + k + 1)
                        if not (first and c == 0):
                            act.wait_ge(thid_done, KR * (t - 1) + k + 1)
                        alone(act)
                        nc.scalar.activation(tgl[:, k, :], p_tg[k][:, 0:S], ACT.Gelu, scale=DOWN,
                                             bias=vcol[:, bass.ds(e * (2 * KR) + KR + k, 1)]).then_inc(tgl_done, 1)
                        if k == 1 and not (last and c + 2 >= W):
                            outx(i, c + 2, first)
                tiles(act, mybir.EngineType.Activation, tileE, 0, E - 1, body)

            @block.vector
            def _(dve):
                def outy(i, c, first):
                    t = W * i + c
                    dve.wait_ge(typ_done, t + 1)
                    if not (first and c < W):
                        dve.wait_ge(t_out[c % W], 32 * (i + c // W))
                    for h in range(2):
                        ins = nc.vector.tensor_scalar(tyo[:, c % W, h, :], p_ty[:, h * P:(h + 1) * P],
                                                      tin[:, c % W, h, P:P + 1], None, ALU.mult)
                    ins.then_inc(ty_done, 1)

                def body(i, c, expert, first, last):
                    t, e = W * i + c, expert[c]
                    for k in range(KR):
                        dve.wait_ge(ta_done, KR * t + k + 1)
                        dve.wait_ge(tgl_done, KR * t + k + 1)
                        if not first:
                            dve.wait_ge(typ_done, t - W + 1)
                        nc.vector.scalar_tensor_tensor(thid[:, c, k, :], p_ta[k][:, 0:S],
                                                       vup[:, bass.ds(e * (2 * KR) + k, 1)], tgl[:, k, :],
                                                       ALU.add, ALU.mult).then_inc(thid_done, 1)
                        if k == 1 and not (first and c == 0):
                            outy(i, c - 1, first)
                    if last and c == W - 1:
                        outy(i, c, first)
                tiles(dve, mybir.EngineType.DVE, tileE, 0, E - 1, body)

            @block.gpsimd
            def _(pool):
                def body(i, c, first, last):
                    pool.wait_ge(ty_done, W * i + c + 1)
                    alone(pool)
                    for h in range(2):
                        pool.indirect_dma_start(
                            out=y_d, out_offset=bass.IndirectOffsetOnAxis(ap=tin[:, c, h, P + 1:P + 2].bitcast(U32), axis=0),
                            in_=tyo[:, c, h, :], in_offset=None, bounds_check=2 * N - 1, oob_is_err=False
                        ).then_inc(t_out[c], 16)
                for c in range(W):
                    body(0, c, True, False)
                with pool.Fori(1, NT // W) as i:
                    for c in range(W):
                        body(i, c, False, False)
                for c in range(W):
                    pool.wait_ge(t_out[c], 32 * (NT // W))

        with nc.Block() as block:
            @block.sync
            def _(sp):
                def load(i, c):
                    g = grp(i, c)
                    if not (isinstance(i, int) and g < 2):
                        sp.wait_ge(sum_done, g - 1)
                    sp.dma_start(ybuf[:, c % 2, :, :, :].rearrange("p j k c -> p j (k c)"),
                                 yg_d[g, :, :, :]).then_inc(y_in[c % 2], 16)

                def store(i, c):
                    g = grp(i, c)
                    sp.wait_ge(sum_done, g + 1)
                    sp.dma_start(og_d[g, :, :, :], acc[:, bass.ds(g * J, J), :]).then_inc(out_done, 16)
                load(0, 0)
                load(0, 1)
                with sp.Fori(1, NG // 2) as i:
                    for c in range(2):
                        load(i, c)
                        store(i, c - 2)
                store(NG // 2 - 1, 0)
                store(NG // 2 - 1, 1)
                sp.wait_ge(out_done, 16 * NG)

            @block.vector
            def _(dve):
                with dve.Fori(0, NG // 2) as i:
                    for c in range(2):
                        g = grp(i, c)
                        at = acc[:, bass.ds(g * J, J), :]
                        dve.wait_ge(y_in[c], 16 * (i + 1))
                        nc.vector.tensor_tensor(at, at, ybuf[:, c, :, 0, :], ALU.add).then_inc(add1, 1)
                        dve.wait_ge(add1, g + 1)
                        nc.vector.tensor_tensor(at, at, ybuf[:, c, :, 1, :], ALU.add).then_inc(sum_done, 1)


_INS = ['x', 'ctx_1024', 'L0_xattn_w', 'L0_xattn_u', 'L0_ffn_Ws1', 'L0_ffn_bs1', 'L0_ffn_Ws2', 'L0_ffn_bs2',
        'L0_ffn_We1', 'L0_ffn_be1', 'L0_ffn_We2', 'L0_ffn_be2', 'L0_ffn_Wr', 'L0_ffn_br']


def kernel(**inputs):
    import numpy as _np
    import concourse.bacc as _bacc
    from concourse import mybir as _mybir
    from concourse.bass_utils import run_bass_kernel_spmd as _run

    nc = _bacc.Bacc("TRN2", target_bir_lowering=False, num_devices=1)
    arrays, args = {}, []
    for name in _INS:
        a = _np.ascontiguousarray(inputs[name])
        arrays[f"in_{name}_dram"] = a
        args.append(nc.dram_tensor(f"in_{name}_dram", a.shape, _mybir.dt.from_np(a.dtype), kind="ExternalInput").ap())
    shape = inputs['x'].shape
    args.append(nc.dram_tensor("out_0_dram", shape, _mybir.dt.float32, kind="ExternalOutput").ap())
    xattn_ffn_kernel(nc, *args)
    r = _run(nc, [arrays], core_ids=[0])
    return r.results[0]["out_0_dram"]
```

```python
from contextlib import ExitStack

import concourse.bass as bass
from concourse import mybir

ALU = mybir.AluOpType
ACT = mybir.ActivationFunctionType
AX = mybir.AxisListType
F32 = mybir.dt.float32
F16 = mybir.dt.float16
BF16 = mybir.dt.bfloat16
I32 = mybir.dt.int32
U32 = mybir.dt.uint32
PE = mybir.EngineType.PE

P = 128
EPS = 1e-5
TAU = 1.5
UP = 256.0
DOWN = 1.0 / UP


def xattn_ffn_kernel(nc, x, ctx_in, w, u, Ws1, bs1, Ws2, bs2, We1, be1, We2, be2, Wr, br, out):
    BATCH, T_LEN, C = x.shape
    E = Wr.shape[1]
    N = BATCH * T_LEN
    G = 1024
    J = G // P
    H = G // 2
    JH = H // P
    NG = N // G
    HS = Ws2.shape[0]
    HR = We2.shape[1]
    KS, KR = HS // P, HR // P
    S = 256
    NT = 2 * N // S + E - 1
    CAP = N + S
    ROW = P + 2
    W = 5
    PADROW = E * CAP
    NOWHERE = 1 << 20
    assert C == P and KR == 3 and KS == 2 and NG % 2 == 0 and E == 12 and H % T_LEN == 0

    xg_d = x.rearrange("b t c -> (b t) c").rearrange("(g j p) c -> g p j c", j=J, p=P)
    cg_d = ctx_in.rearrange("b t c -> (b t) c").rearrange("(g j p) c -> g p j c", j=J, p=P)
    og_d = out.rearrange("b t c -> (b t) c").rearrange("(g j p) c -> g p j c", j=J, p=P)
    sorted_d = nc.dram_tensor("sorted_rows", (E * CAP + S, ROW), F32, kind="Internal").ap()
    parts_d = nc.dram_tensor("bias_parts", (3, (E + 1) * C), BF16, kind="Internal").ap()
    y_d = nc.dram_tensor("expert_out", (2 * N, P), F32, kind="Internal").ap()
    yg_d = y_d.rearrange("(g j p k) c -> g p j (k c)", j=J, p=P, k=2)

    with ExitStack() as ctx:
        def sb(name, shape, dt):
            return ctx.enter_context(nc.sbuf_tensor(name, shape, dt))

        def ps(name, shape, dt):
            return ctx.enter_context(nc.psum_tensor(name, shape, dt))

        def sem(name):
            return ctx.enter_context(nc.semaphore(name))

        acc = sb("acc", [P, NG * J, C], F32)
        w1h = sb("w1h", [P, E * 2 * HR], F16)
        w1l = sb("w1l", [P, E * 2 * HR], F16)
        w2 = sb("w2", [P, E * KR, C], F32)
        s1f = sb("s1f", [P, 2 * HS], F32)
        s1h = sb("s1h", [P, 2 * HS], F16)
        s1l = sb("s1l", [P, 2 * HS], F16)
        s2 = sb("s2", [P, KS, C], F32)
        wrf = sb("wrf", [P, E], F32)
        wrh = sb("wrh", [P, E], F16)
        wrl = sb("wrl", [P, E], F16)
        brb = sb("brb", [P, E], F32)
        NB = E * 2 * KR + 2 * KS + 2
        WROW, UROW = NB - 2, NB - 1
        vrow = sb("vrow", [NB, P], F32)
        vcol = sb("vcol", [P, NB], F32)
        vup = sb("vup", [P, NB], F32)
        b2s = sb("b2s", [3, (E + 1) * C], BF16)
        ewu = sb("ewu", [P, 2], F32)
        decay = sb("decay", [P, 2 * H + 1], F32)
        identf = sb("identf", [P, P], F32)
        identh = sb("identh", [P, P], F16)
        diagu = sb("diagu", [P, P], F32)
        before = sb("before", [P, P], BF16)
        ones = sb("ones", [P, P], BF16)
        epsc = sb("epsc", [P, 1], F32)
        scale1 = sb("scale1", [P, NG * J], F32)
        bias1 = sb("bias1", [P, NG * J], F32)
        eidx = sb("eidx", [P, E], F32)
        ebase = sb("ebase", [P, E], F32)
        hist = sb("hist", [P, E], BF16)
        dest = sb("dest", [P, J, 2], F32)
        pad = sb("pad", [P, 2, ROW], F32)
        counts = sb("counts", [P, E], F32)
        tabi = sb("tabi", [P, 2, E], I32)
        tab = sb("tab", [P, 6, E], F32)
        tcol = sb("tcol", [P, 6], F32)
        tileno = sb("tileno", [P, 1], F32)
        tileE = sb("tileE", [1, NT // W, 8], I32)
        tileR = sb("tileR", [1, NT // W, 8], I32)
        padat = sb("padat", [1, E], I32)

        ct = sb("ct", [P, 2, J, C], F32)
        ek = sb("ek", [P, 2, 2, 2, H], F32)
        fw = sb("fw", [P, 2, 2 * H + 1], F32)
        bw = sb("bw", [P, 2, 2 * H + 1], F32)
        nsig = sb("nsig", [P, 2, J, C], F32)
        dens = sb("dens", [P, H], F32)
        rcp = sb("rcp", [P, H], F32)
        lnl = sb("lnl", [P, J], F32)
        bns = sb("bns", [P, J, 6], F32)
        mv = sb("mv", [P, J, 2], F32)
        lnv = sb("lnv", [P, J], F32)
        lnr = sb("lnr", [P, J], F32)
        lnm = sb("lnm", [P, J], F32)
        lng = sb("lng", [P, J], F32)
        lnscale = sb("lnscale", [P, J], F32)
        lnbias = sb("lnbias", [P, J], F32)
        xn = sb("xn", [P, J, C], F32)
        rows = sb("rows", [P, 2, J, 2, ROW], F32)
        xT = sb("xT", [P, 2, 2, H], F16)
        gl = sb("gl", [P, KS, H], F32)
        hid = sb("hid", [P, 2, KS, H], F32)
        wst = sb("wst", [P, 2, 2 * HR], F32)
        lg = sb("lg", [P, J, E], F32)
        top = sb("top", [P, J, 8], F32)
        topi = sb("topi", [P, J, 8], U32)
        oneh = sb("oneh", [P, J, 2, E], F32)
        both = sb("both", [P, J, E], BF16)
        seen = sb("seen", [P, E], F32)
        diff = sb("diff", [P, J], F32)
        ediff = sb("ediff", [P, J], F32)
        wsum = sb("wsum", [P, J], F32)
        wfirst = sb("wfirst", [P, J], F32)
        place = sb("place", [P, J, E], F32)
        placed = sb("placed", [P, J, 2, E], F32)
        slot = sb("slot", [P, 2, J, 2], U32)

        hidw = hid[:, :, :, :].rearrange("p a k n -> p (a k n)")
        b2f = hidw[0:E + 1, 0:C]
        b2r = hidw[0:E + 1, C:2 * C]
        b2t = hidw[0:E + 1, 2 * C:4 * C].bitcast(BF16)[:, 0:3 * C].rearrange("p (m c) -> p m c", m=3)
        batches = [(0, 1), (1, NG // 2), (NG // 2, NG)]
        tiles1 = [(b1 - b0) * J for b0, b1 in batches]
        first = [hidw[:, 4 * C + 13 * b0 * J:4 * C + 13 * b1 * J] for b0, b1 in batches]
        bns1 = [f[:, 0:6 * n].rearrange("p (t k) -> p t k", k=6) for f, n in zip(first, tiles1)]
        mv1 = [f[:, 6 * n:8 * n].rearrange("p (t k) -> p t k", k=2) for f, n in zip(first, tiles1)]
        lnl1, lng1, lnv1, lnm1, lnr1 = ([f[:, (8 + k) * n:(9 + k) * n] for f, n in zip(first, tiles1)] for k in range(5))
        assert NT <= P and 4 * C + 13 * NG * J <= 2 * KS * H

        ctw = ct[:, :, :, :].rearrange("p a j c -> p (a j c)")
        tin = ctw[:, 0:W * 2 * ROW].rearrange("p (s h r) -> p s h r", s=W, h=2)
        txT = hidw[:, 0:W * S].bitcast(F16).rearrange("p (s l n) -> p s l n", s=W, l=2)
        fww = fw[:, :, :].rearrange("p a n -> p (a n)")
        tgl = fww[:, 0:KR * S].rearrange("p (k n) -> p k n", k=KR)
        nsigw = nsig[:, :, :, :].rearrange("p a j c -> p (a j c)")
        tyo = nsigw[:, 0:W * S].rearrange("p (s h c) -> p s h c", s=W, h=2)
        ekw = ek[:, :, :, :, :].rearrange("p a h v n -> p (a h v n)")
        thid = ekw[:, 0:W * KR * S].rearrange("p (s k n) -> p s k n", s=W, k=KR)
        ybuf = ekw.rearrange("p (s j k c) -> p s j k c", s=2, j=J, k=2)

        p_ct = ps("p_ct", [P, H], F32)
        p_num = ps("p_num", [P, H], F32)
        p_den = ps("p_den", [P, H], F32)
        p_xT = ps("p_xT", [P, 2, H], F16)
        p_rt = ps("p_rt", [P, 512], F32)
        p_g = ps("p_g", [P, H], F32)
        p_a = ps("p_a", [P, H], F32)
        p_y = ps("p_y", [P, H], F32)
        p_xTf = p_xT[:, :, :].rearrange("p a n -> p (a n)").bitcast(F32)
        p_lg = p_rt[:, 0:J * E]
        p_pf = p_rt[:, 128:128 + J * E]
        p_cnt = p_rt[:, 256:256 + E]
        p_vec = p_rt[:, 384:384 + NB]
        p_tile = p_rt[0:1, 0:2 * P]
        p_tg = [p_ct, p_num, p_den]
        p_ta = [p_g, p_a, p_rt]
        p_tx = p_xT
        p_ty = p_y

        passed = sem("passed")
        x_in = [sem(f"x_in{b}") for b in range(3)]
        first_bn = sem("first_bn")
        first_mv = sem("first_mv")
        first_ln = sem("first_ln")
        first_guess = sem("first_guess")
        first_step = sem("first_step")
        parts_out = sem("parts_out")
        ctx_ld = [sem(f"ctx_ld{k}") for k in range(2)]
        w_ld = [sem(f"w_ld{k}") for k in range(2)]
        sw_in = sem("sw_in")
        w2_in = sem("w2_in")
        parts_in = sem("parts_in")
        pad_out = sem("pad_out")
        scat = [sem(f"scat{k}") for k in range(2)]
        pool_const = sem("pool_const")
        dve_const = sem("dve_const")
        act_const = sem("act_const")
        pe_const = sem("pe_const")
        ctxT_done = sem("ctxT_done")
        ek_done = sem("ek_done")
        ekv_done = sem("ekv_done")
        scan_done = sem("scan_done")
        swept = sem("swept")
        dp_done = sem("dp_done")
        np_done = sem("np_done")
        den_done = sem("den_done")
        rden_done = sem("rden_done")
        newton = sem("newton")
        quo_done = sem("quo_done")
        x2_done = sem("x2_done")
        bn_done = sem("bn_done")
        mv_done = sem("mv_done")
        ln_step = sem("ln_step")
        guess_done = sem("guess_done")
        lnl_done = sem("lnl_done")
        dln_done = sem("dln_done")
        nsig_done = sem("nsig_done")
        xn_done = sem("xn_done")
        hi_done = sem("hi_done")
        lo_done = sem("lo_done")
        rows_done = sem("rows_done")
        xTp_done = sem("xTp_done")
        xT_done = sem("xT_done")
        lgp_done = sem("lgp_done")
        rt_step = sem("rt_step")
        both_done = sem("both_done")
        pf_done = sem("pf_done")
        diff_done = sem("diff_done")
        ediff_done = sem("ediff_done")
        wsum_done = sem("wsum_done")
        meta_done = sem("meta_done")
        slot_done = sem("slot_done")
        upg_done = sem("upg_done")
        upa_done = sem("upa_done")
        gl_done = sem("gl_done")
        hid_done = sem("hid_done")
        yp_done = sem("yp_done")
        acc_done = sem("acc_done")
        whi_done = sem("whi_done")
        wlo_done = sem("wlo_done")
        cnt_done = sem("cnt_done")
        tab_step = sem("tab_step")
        tcol_done = sem("tcol_done")
        trow_done = sem("trow_done")
        tab_done = sem("tab_done")
        padded = sem("padded")
        t_in = [sem(f"t_in{k}") for k in range(W)]
        t_out = [sem(f"t_out{k}") for k in range(W)]
        txp_done = sem("txp_done")
        tx_done = sem("tx_done")
        tg_done = sem("tg_done")
        ta_done = sem("ta_done")
        tgl_done = sem("tgl_done")
        thid_done = sem("thid_done")
        typ_done = sem("typ_done")
        ty_done = sem("ty_done")
        y_in = [sem(f"y_in{k}") for k in range(2)]
        add1 = sem("add1")
        sum_done = sem("sum_done")
        out_done = sem("out_done")

        SW_LOADS, POOL_CONSTS, DVE_CONSTS, META, TABS = 16 * 10, 18, 11, 4, 4
        LNS = 7

        def grp(i, c):
            return 2 * i + c

        def turn(i, c):
            return i + c // 2 + 1

        def steps(eng, body):
            for i in range(2):
                body(i, 0)
                body(i, 1)
            with eng.Fori(2, NG // 2) as i:
                body(i, 0)
                body(i, 1)
            body(NG // 2, 0)
            body(NG // 2, 1)

        def stages(i, c):
            if isinstance(i, int):
                s = grp(i, c)
                return s < NG, 1 <= s <= NG, 2 <= s <= NG + 1, 3 <= s
            return True, True, True, True

        def experts(i, c):
            when = {0: (0, 1), 1: (2, 3), 2: (4, 5), 3: (6, 7), NG: (8, 9), NG + 1: (10, 11)}
            return when.get(grp(i, c), ()) if isinstance(i, int) else ()

        def ifat(eng, i, c, back, sm, value):
            if not isinstance(i, int) or grp(i, c) >= back:
                eng.wait_ge(sm, value)

        def alone(eng):
            eng.sem_inc(passed, 1)

        with nc.Block() as block:
            @block.sync
            def _(sp):
                def loads(i, c):
                    if not stages(i, c)[0]:
                        return
                    k, g = c % 2, grp(i, c)
                    ifat(sp, i, c, 2, ctxT_done, 2 * (g - 2) + 2)
                    sp.dma_start(ct[:, k, :, :], cg_d[g, :, :, :]).then_inc(ctx_ld[k], 16)

                def weights(i, c):
                    for e in experts(i, c):
                        if e >= 2:
                            sp.wait_ge(wlo_done, e - 1)
                        sp.dma_start(wst[:, e % 2, :], We1[e, :, :]).then_inc(w_ld[e % 2], 16)

                sp.dma_start(vrow[0:E * 2 * KR, :], be1.rearrange("e (k p) -> (e k) p", p=P)).then_inc(sw_in, 16)
                sp.dma_start(vrow[E * 2 * KR:WROW, :], bs1.rearrange("(k p) -> k p", p=P)).then_inc(sw_in, 16)
                sp.dma_start(vrow[WROW:UROW, :], w[0, :, :]).then_inc(sw_in, 16)
                sp.dma_start(vrow[UROW:NB, :], u[0, :, :]).then_inc(sw_in, 16)
                sp.dma_start(b2f[0:E, :], be2).then_inc(sw_in, 16)
                sp.dma_start(b2f[E:E + 1, :], bs2.rearrange("(a c) -> a c", a=1)).then_inc(sw_in, 16)
                sp.dma_start(brb[:, :], br.partition_broadcast(P)).then_inc(sw_in, 16)
                sp.dma_start(wrf[:, :], Wr).then_inc(sw_in, 16)
                sp.dma_start(s1f[:, :], Ws1).then_inc(sw_in, 16)
                sp.dma_start(s2[:, :, :], Ws2.rearrange("(k p) d -> p k d", p=P)).then_inc(sw_in, 16)

                def body(i, c):
                    loads(i, c)
                    if isinstance(i, int) and grp(i, c) in (0, 1):
                        for b in ((0, 1), (2,))[grp(i, c)]:
                            for g in range(*batches[b]):
                                sp.dma_start(acc[:, g * J:(g + 1) * J, :], xg_d[g, :, :, :]).then_inc(x_in[b], 16)
                    weights(i, c)
                    if isinstance(i, int) and grp(i, c) == 1:
                        sp.wait_ge(dve_const, DVE_CONSTS)
                        sp.dma_start(parts_d.rearrange("m (e c) -> e m c", c=C), b2t[:, :, :]).then_inc(parts_out, 16)
                        sp.wait_ge(pool_const, POOL_CONSTS)
                        sp.dma_start(sorted_d[PADROW:PADROW + S, :].rearrange("(h p) r -> p h r", p=P),
                                     pad[:, :, :]).then_inc(pad_out, 16)
                        sp.wait_ge(parts_out, 16)
                        sp.dma_start(b2s[:, :], parts_d).then_inc(parts_in, 16)
                    if isinstance(i, int) and grp(i, c) == 2:
                        sp.dma_start(w2[:, :, :], We2.rearrange("e (k p) d -> p (e k) d", p=P)).then_inc(w2_in, 16)
                steps(sp, body)
                sp.wait_ge(tab_done, 1)
                ends = nc.values_load_multi_w_load_instructions(
                    padat[0:1, :], engines=[mybir.EngineType.SP], min_val=0, max_val=PADROW - S,
                    skip_runtime_bounds_check_because="a region's first row and a count of at most N rows")[1]
                for e in range(E):
                    sp.dma_start(sorted_d[bass.ds(ends[e], S), :].rearrange("(h p) r -> p h r", p=P),
                                 pad[:, :, :]).then_inc(padded, 16)
                sp.wait_ge(pad_out, 16)
                sp.wait_ge(padded, 16 * E)
                sp.wait_ge(w2_in, 16)
                for k in range(2):
                    sp.wait_ge(scat[k], 16 * 2 * J * (NG // 2))

            @block.gpsimd
            def _(pool):
                n = [0]

                def const(ins):
                    n[0] += 1
                    ins.then_inc(pool_const, 1)

                def behind(ins):
                    pool.wait_ge(pool_const, n[0])
                    const(ins())

                const(nc.gpsimd.memset(identf[:, :], 0.0))
                behind(lambda: nc.gpsimd.affine_select(out=identf[:, :], in_=identf[:, :], compare_op=ALU.not_equal,
                                                       fill=1.0, base=0, pattern=[[-1, P]], channel_multiplier=1))
                const(nc.gpsimd.memset(identh[:, :], 0.0))
                behind(lambda: nc.gpsimd.affine_select(out=identh[:, :], in_=identh[:, :], compare_op=ALU.not_equal,
                                                       fill=1.0, base=0, pattern=[[-1, P]], channel_multiplier=1))
                const(nc.gpsimd.memset(ones[:, :], 1.0))
                const(nc.gpsimd.memset(before[:, :], 1.0))
                behind(lambda: nc.gpsimd.affine_select(out=before[:, :], in_=before[:, :], compare_op=ALU.is_ge,
                                                       fill=0.0, base=-1, pattern=[[1, P]], channel_multiplier=-1))
                const(nc.gpsimd.memset(epsc[:, :], EPS))
                const(nc.gpsimd.memset(hist[:, :], 0.0))
                const(nc.gpsimd.iota(eidx[:, :], pattern=[[1, E]], base=0, channel_multiplier=0,
                                     allow_small_or_imprecise_dtypes=True))
                const(nc.gpsimd.iota(ebase[:, :], pattern=[[CAP, E]], base=0, channel_multiplier=0,
                                     allow_small_or_imprecise_dtypes=True))
                const(nc.gpsimd.iota(dest[:, :, :], pattern=[[2 * P, J], [1, 2]], base=0, channel_multiplier=2,
                                     allow_small_or_imprecise_dtypes=True))
                const(nc.gpsimd.iota(tileno[:, :], pattern=[[1, 1]], base=0, channel_multiplier=1,
                                     allow_small_or_imprecise_dtypes=True))
                const(nc.gpsimd.memset(pad[:, :, :], 0.0))
                behind(lambda: nc.gpsimd.memset(pad[:, :, P + 1:P + 2].bitcast(I32), NOWHERE))
                for h in range(2):
                    const(nc.gpsimd.memset(fw[:, h, 0:1], 0.0))
                const(nc.gpsimd.memset(bw[:, :, 2 * H:2 * H + 1], 0.0))
                assert n[0] == POOL_CONSTS

                def chain(sm, base, stat, guessed, v, m, r, guess, scale, bias, sign, free):
                    def small(n, out, in0, in1):
                        if not (isinstance(base, int) and base == 0 and n == 0):
                            pool.wait_ge(sm, base + n)
                            alone(pool)
                        if isinstance(in1, tuple):
                            ins = nc.gpsimd.tensor_scalar(out, in0, in1[0], in1[1], *in1[2:])
                        else:
                            ins = nc.gpsimd.tensor_tensor(out, in0, in1, ALU.mult)
                        ins.then_inc(sm, 1)
                    small(0, v, stat[:, :, 1], (EPS, None, ALU.add))
                    small(1, m, stat[:, :, 0], (-1.0, None, ALU.mult))
                    guessed()
                    small(2, r, guess, guess)
                    small(3, r, r, v)
                    small(4, r, r, (-0.5 * sign, 1.5 * sign, ALU.mult, ALU.add))
                    free()
                    small(5, scale, r, guess)
                    small(6, bias, scale, m)

                def firstnorm(b):
                    pool.wait_ge(first_mv, b + 1)
                    alone(pool)

                    def guessed():
                        pool.wait_ge(first_guess, b + 1)
                        alone(pool)
                    of = slice(batches[b][0] * J, batches[b][1] * J)
                    chain(first_step, LNS * b, mv1[b], guessed, lnv1[b], lnm1[b], lnr1[b], lng1[b],
                          scale1[:, of], bias1[:, of], -1.0, lambda: None)

                def secondnorm(i, c):
                    g = grp(i, c)
                    pool.wait_ge(mv_done, g + 1)
                    alone(pool)

                    def guessed():
                        pool.wait_ge(guess_done, g + 1)
                        alone(pool)

                    def free():
                        if not isinstance(i, int) or g >= 1:
                            pool.wait_ge(xn_done, g)
                            alone(pool)
                    chain(ln_step, LNS * g, mv, guessed, lnv[:, :], lnm[:, :], lnr[:, :], lng[:, :],
                          lnscale[:, :], lnbias[:, :], 1.0, free)

                def low(i, c):
                    k, g = c % 2, grp(i, c)
                    pool.wait_ge(hi_done, g + 1)
                    alone(pool)
                    nc.gpsimd.tensor_tensor(rows[:, k, :, 0, C // 2:C].bitcast(F16), xn[:, :, :],
                                            rows[:, k, :, 0, 0:C // 2].bitcast(F16), ALU.subtract).then_inc(lo_done, 1)

                def dispatch(i, c):
                    k, g = c % 2, grp(i, c)
                    pool.wait_ge(slot_done, g + 1)
                    alone(pool)
                    pool.wait_ge(meta_done, META * (g + 1))
                    alone(pool)
                    pool.wait_ge(rows_done, g + 1)
                    alone(pool)
                    for j in range(J):
                        for m in range(2):
                            pool.indirect_dma_start(
                                out=sorted_d, out_offset=bass.IndirectOffsetOnAxis(ap=slot[:, k, j, m:m + 1], axis=0),
                                in_=rows[:, k, j, m, :], in_offset=None).then_inc(scat[k], 16)

                def body(i, c):
                    begin, end, ffn, tail = stages(i, c)
                    if isinstance(i, int) and grp(i, c) == 0:
                        firstnorm(0)
                        firstnorm(1)
                    if end:
                        secondnorm(i, c - 1)
                        low(i, c - 1)
                    if isinstance(i, int) and grp(i, c) == 1:
                        firstnorm(2)
                    if ffn:
                        dispatch(i, c - 2)
                steps(pool, body)

            @block.scalar
            def _(act):
                nc.scalar.preload_act_table_set("natural_log_exp_and_others")
                act.wait_ge(sw_in, SW_LOADS)
                nc.scalar.activation(s1h[:, :], s1f[:, :], ACT.Copy, scale=UP).then_inc(act_const, 1)
                nc.scalar.activation(wrh[:, :], wrf[:, :], ACT.Copy, scale=UP).then_inc(act_const, 1)
                act.wait_ge(pe_const, 1)
                nc.scalar.activation(vcol[:, :], p_vec, ACT.Copy).then_inc(act_const, 1)
                act.wait_ge(act_const, 3)
                nc.scalar.activation(ewu[:, :], vcol[:, WROW:NB], ACT.Exp).then_inc(act_const, 1)

                def exps(i, c, h):
                    g = grp(i, c)
                    act.wait_ge(ctxT_done, 2 * g + h + 1)
                    ifat(act, i, c, 2, np_done, 2 * (g - 2) + h + 1)
                    nc.scalar.activation(ek[:, c % 2, h, 1, :], p_ct[:, :], ACT.Exp).then_inc(ek_done, 1)

                def reciprocal(i, c, h):
                    n = 2 * grp(i, c) + h
                    act.wait_ge(den_done, n + 1)
                    if not (isinstance(i, int) and n == 0):
                        act.wait_ge(x2_done, n)
                    nc.scalar.activation(rcp[:, :], dens[:, :], ACT.Ln).then_inc(dln_done, 1)
                    act.wait_ge(dln_done, n + 1)
                    nc.scalar.activation(rcp[:, :], rcp[:, :], ACT.Exp, scale=-1.0).then_inc(rden_done, 1)

                def outx(i, c, h):
                    g = grp(i, c)
                    act.wait_ge(xTp_done, 2 * g + h + 1)
                    ifat(act, i, c, 1, upa_done, 4 * (g - 1) + 2 * h + 2)
                    ifat(act, i, c, 1, lgp_done, g)
                    nc.scalar.activation(xT[:, h, :, :], p_xT[:, :, :], ACT.Copy).then_inc(xT_done, 1)

                def gelu(i, c, h, f):
                    n = 4 * grp(i, c) + 2 * h + f
                    act.wait_ge(upg_done, n + 1)
                    if not (isinstance(i, int) and n <= 1):
                        act.wait_ge(hid_done, n - 1)
                    nc.scalar.activation(gl[:, f, :], (p_g, p_ct)[f][:, :], ACT.Gelu, scale=DOWN,
                                         bias=vcol[:, E * 2 * KR + KS + f:E * 2 * KR + KS + f + 1]).then_inc(gl_done, 1)

                def weigh(i, c):
                    g = grp(i, c)
                    act.wait_ge(diff_done, g + 1)
                    ifat(act, i, c, 1, meta_done, META * g)
                    nc.scalar.activation(ediff[:, :], diff[:, :], ACT.Exp, scale=1.0 / TAU).then_inc(ediff_done, 1)

                def firstguess(b):
                    act.wait_ge(first_mv, b + 1)
                    nc.scalar.activation(lnl1[b], mv1[b][:, :, 1], ACT.Ln, bias=epsc[:, 0:1]).then_inc(first_ln, 1)
                    act.wait_ge(first_ln, b + 1)
                    nc.scalar.activation(lng1[b], lnl1[b], ACT.Exp, scale=-0.5).then_inc(first_guess, 1)

                def guess(i, c):
                    g = grp(i, c)
                    act.wait_ge(mv_done, g + 1)
                    ifat(act, i, c, 1, ln_step, LNS * g)
                    nc.scalar.activation(lnl[:, :], mv[:, :, 1], ACT.Ln, bias=epsc[:, 0:1]).then_inc(lnl_done, 1)
                    act.wait_ge(lnl_done, g + 1)
                    nc.scalar.activation(lng[:, :], lnl[:, :], ACT.Exp, scale=-0.5).then_inc(guess_done, 1)

                def weights(i, c):
                    for e in experts(i, c):
                        act.wait_ge(w_ld[e % 2], 16 * (e // 2 + 1))
                        nc.scalar.activation(w1h[:, e * 2 * HR:(e + 1) * 2 * HR], wst[:, e % 2, :], ACT.Copy,
                                             scale=UP).then_inc(whi_done, 1)

                def sigmoids(i, c):
                    k, g = c % 2, grp(i, c)
                    for b in range(3):
                        if isinstance(i, int) and g == batches[b][0]:
                            act.wait_ge(first_step, LNS * (b + 1))
                    ifat(act, i, c, 2, den_done, 2 * (g - 2) + 2)
                    alone(act)
                    for j in range(J):
                        ins = nc.scalar.activation(nsig[:, k, j, :], acc[:, g * J + j, :], ACT.Exp,
                                                   scale=scale1[:, bass.ds(g * J + j, 1)],
                                                   bias=bias1[:, bass.ds(g * J + j, 1)])
                    ins.then_inc(nsig_done, 1)

                def normed(i, c):
                    k, g = c % 2, grp(i, c)
                    act.wait_ge(ln_step, LNS * (g + 1))
                    ifat(act, i, c, 1, lo_done, g)
                    alone(act)
                    for j in range(J):
                        ins = nc.scalar.activation(xn[:, j, :], acc[:, g * J + j, :], ACT.Identity,
                                                   scale=lnscale[:, j:j + 1], bias=lnbias[:, j:j + 1])
                    ins.then_inc(xn_done, 1)

                def high(i, c):
                    k, g = c % 2, grp(i, c)
                    act.wait_ge(xn_done, g + 1)
                    ifat(act, i, c, 2, xTp_done, 2 * (g - 2) + 2)
                    ifat(act, i, c, 2, scat[k], 16 * 2 * J * (turn(i, c) - 1))
                    alone(act)
                    nc.scalar.activation(rows[:, k, :, 0, 0:C // 2].bitcast(F16), xn[:, :, :],
                                         ACT.Copy).then_inc(hi_done, 1)

                def body(i, c):
                    begin, end, ffn, tail = stages(i, c)
                    if end:
                        reciprocal(i, c - 1, 1)
                    if begin:
                        exps(i, c, 0)
                    if ffn:
                        outx(i, c - 2, 0)
                        outx(i, c - 2, 1)
                    if begin:
                        exps(i, c, 1)
                    weights(i, c)
                    if end:
                        guess(i, c - 1)
                    if isinstance(i, int) and grp(i, c) == 0:
                        firstguess(0)
                    if begin:
                        sigmoids(i, c)
                    if end:
                        normed(i, c - 1)
                    if end:
                        high(i, c - 1)
                    if ffn:
                        weigh(i, c - 2)
                    if begin:
                        reciprocal(i, c, 0)
                    if isinstance(i, int) and grp(i, c) in (0, 1):
                        firstguess(grp(i, c) + 1)
                    if ffn:
                        nc.scalar.preload_act_table_set("gelu_and_others")
                        gelu(i, c - 2, 0, 0)
                        gelu(i, c - 2, 0, 1)
                        gelu(i, c - 2, 1, 0)
                        gelu(i, c - 2, 1, 1)
                        if end:
                            nc.scalar.preload_act_table_set("natural_log_exp_and_others")
                steps(act, body)

            @block.vector
            def _(dve):
                n = [0]

                def const(ins, wait=True):
                    n[0] += 1
                    ins.then_inc(dve_const, 1)
                    if wait:
                        dve.wait_ge(dve_const, n[0])

                dve.wait_ge(sw_in, SW_LOADS)
                dve.wait_ge(act_const, 4)
                dve.wait_ge(pool_const, POOL_CONSTS)
                const(nc.vector.tensor_copy(decay[:, :], ewu[:, 0:1].to_broadcast([P, 2 * H + 1])))
                const(nc.vector.memset(decay[:, 0:2 * H + 1:T_LEN], 0.0), False)
                const(nc.vector.tensor_scalar(diagu[:, :], identf[:, :], ewu[:, 1:2], None, ALU.mult), False)
                const(nc.vector.tensor_scalar(vup[:, :], vcol[:, :], UP, None, ALU.mult), False)
                const(nc.vector.scalar_tensor_tensor(s1l[:, :], s1f[:, :], UP, s1h[:, :], ALU.mult, ALU.subtract), False)
                const(nc.vector.scalar_tensor_tensor(wrl[:, :], wrf[:, :], UP, wrh[:, :], ALU.mult, ALU.subtract), False)
                const(nc.vector.tensor_scalar(b2r[:, :], b2f[:, :], UP, None, ALU.mult))
                const(nc.vector.tensor_copy(b2t[:, 0, :], b2r[:, :]))
                const(nc.vector.tensor_tensor(b2f[:, :], b2r[:, :], b2t[:, 0, :], ALU.subtract))
                const(nc.vector.tensor_copy(b2t[:, 1, :], b2f[:, :]))
                const(nc.vector.tensor_tensor(b2t[:, 2, :], b2f[:, :], b2t[:, 1, :], ALU.subtract))
                assert n[0] == DVE_CONSTS
                def ekv(i, c, h):
                    g = grp(i, c)
                    dve.wait_ge(ek_done, 2 * g + h + 1)
                    nc.vector.tensor_tensor(ek[:, c % 2, h, 0, :], ek[:, c % 2, h, 1, :], p_ct[:, :],
                                            ALU.mult).then_inc(ekv_done, 1)

                def scan(i, c, h):
                    g = grp(i, c)
                    dve.wait_ge(ekv_done, 2 * g + h + 1)
                    ifat(dve, i, c, 1, np_done, 2 * (g - 1) + h + 1)
                    src = ek[:, c % 2, h, :, :].rearrange("p v n -> p (v n)")
                    nc.vector.tensor_tensor_scan(fw[:, h, 1:2 * H + 1], decay[:, 0:2 * H], src, 0.0,
                                                 ALU.mult, ALU.add).then_inc(swept, 1)
                    nc.vector.tensor_tensor_scan(back(bw[:, h, 0:2 * H]), back(decay[:, 1:2 * H + 1]), back(src), 0.0,
                                                 ALU.mult, ALU.add).then_inc(swept, 1)

                def cutoff(i, c, h):
                    g = grp(i, c)
                    dve.wait_ge(swept, 4 * g + 2 * h + 2)
                    nc.vector.memset(fw[:, h, T_LEN:2 * H + 1:T_LEN], 0.0)
                    nc.vector.memset(bw[:, h, 0:2 * H:T_LEN], 0.0).then_inc(scan_done, 1)

                def back(a):
                    p, (_, m) = a.ap[0], a.ap[-1]
                    return bass.AP(a.tensor, a.offset + m - 1, [list(p), [-1, m]])

                def den(i, c, h):
                    k, g = c % 2, grp(i, c)
                    dve.wait_ge(dp_done, 2 * g + h + 1)
                    dve.wait_ge(nsig_done, g + 1)
                    if not (isinstance(i, int) and g == 0 and h == 0):
                        dve.wait_ge(x2_done, 2 * g + h)
                    nc.vector.scalar_tensor_tensor(dens[:, :], nsig[:, k, h * JH:(h + 1) * JH, :].rearrange("p j c -> p (j c)"),
                                                   1.0, p_den[:, :], ALU.add, ALU.mult).then_inc(den_done, 1)

                def quotient(i, c, h):
                    g = grp(i, c)
                    n = 2 * g + h
                    dve.wait_ge(rden_done, n + 1)
                    dve.wait_ge(np_done, n + 1)
                    nc.vector.tensor_tensor(dens[:, :], dens[:, :], rcp[:, :], ALU.mult).then_inc(newton, 1)
                    nc.vector.tensor_tensor(rcp[:, :], p_num[:, :], rcp[:, :], ALU.mult).then_inc(quo_done, 1)

                def refine(i, c, h):
                    g = grp(i, c)
                    n = 2 * g + h
                    dve.wait_ge(quo_done, n + 1)
                    nc.vector.scalar_tensor_tensor(rcp[:, :], dens[:, :], 2.0, rcp[:, :], ALU.subtract, ALU.mult).then_inc(newton, 1)

                def add(i, c, h):
                    g = grp(i, c)
                    n = 2 * g + h
                    dve.wait_ge(newton, 2 * n + 2)
                    at = acc[:, bass.ds(g * J + h * JH, JH), :].rearrange("p j c -> p (j c)")
                    nc.vector.tensor_tensor(at, at, rcp[:, :], ALU.subtract).then_inc(x2_done, 1)

                def geglu(i, c, h, f):
                    g = grp(i, c)
                    n = 4 * g + 2 * h + f
                    dve.wait_ge(upa_done, n + 1)
                    dve.wait_ge(gl_done, n + 1)
                    ifat(dve, i, c, 1, yp_done, 2 * (g - 1) + h + 1)
                    if isinstance(i, int) and n == 0:
                        dve.wait_ge(parts_out, 16)
                        dve.wait_ge(first_step, 3 * LNS)
                    nc.vector.scalar_tensor_tensor(hid[:, h, f, :], (p_a, p_xTf)[f][:, :], vup[:, E * 2 * KR + f:E * 2 * KR + f + 1],
                                                   gl[:, f, :], ALU.add, ALU.mult).then_inc(hid_done, 1)

                def addffn(i, c, h):
                    g = grp(i, c)
                    dve.wait_ge(yp_done, 2 * g + h + 1)
                    at = acc[:, bass.ds(g * J + h * JH, JH), :].rearrange("p j c -> p (j c)")
                    nc.vector.scalar_tensor_tensor(at, p_y[:, :], DOWN, at, ALU.mult, ALU.add).then_inc(acc_done, 1)

                def logits(i, c):
                    g = grp(i, c)
                    dve.wait_ge(lgp_done, g + 1)
                    ifat(dve, i, c, 1, rt_step, 5 * g)
                    ifat(dve, i, c, 1, tab_step, TABS * g)
                    ifat(dve, i, c, 1, meta_done, META * g)
                    nc.vector.scalar_tensor_tensor(lg[:, :, :], p_lg.rearrange("p (j e) -> p j e", e=E), DOWN,
                                                   brb[:, None, :].to_broadcast([P, J, E]), ALU.mult, ALU.add).then_inc(rt_step, 1)

                def best(i, c):
                    g = grp(i, c)
                    dve.wait_ge(rt_step, 5 * g + 1)
                    alone(dve)
                    for j in range(J):
                        ins = nc.vector.max(top[:, j, :], lg[:, j, :])
                    ins.then_inc(rt_step, 1)

                def which(i, c):
                    g = grp(i, c)
                    dve.wait_ge(rt_step, 5 * g + 2)
                    alone(dve)
                    for j in range(J):
                        ins = nc.vector.max_index(topi[:, j, :], top[:, j, :], lg[:, j, :])
                    ifat(dve, i, c, 1, ediff_done, g)
                    nc.vector.tensor_tensor(diff[:, :], top[:, :, 1], top[:, :, 0], ALU.subtract).then_inc(diff_done, 1)
                    ins.then_inc(rt_step, 1)
                    dve.wait_ge(rt_step, 5 * g + 3)
                    nc.vector.tensor_tensor(oneh[:, :, :, :], topi[:, :, 0:2, None].to_broadcast([P, J, 2, E]),
                                            eidx[:, None, None, :].to_broadcast([P, J, 2, E]),
                                            ALU.is_equal).then_inc(rt_step, 1)
                    dve.wait_ge(rt_step, 5 * g + 4)
                    ifat(dve, i, c, 1, pf_done, g)
                    nc.vector.tensor_tensor(both[:, :, :], oneh[:, :, 0, :], oneh[:, :, 1, :], ALU.add).then_inc(both_done, 1)

                def assign(i, c):
                    k, g = c % 2, grp(i, c)
                    meta = rows[:, k, :, :, :]
                    dve.wait_ge(pf_done, g + 1)
                    nc.vector.tensor_tensor(place[:, :, :], p_pf.rearrange("p (j e) -> p j e", e=E),
                                            ebase[:, None, :].to_broadcast([P, J, E]), ALU.add).then_inc(rt_step, 1)
                    nc.vector.tensor_reduce(seen[:, :], both[:, :, :].rearrange("p j e -> p e j"), AX.X, ALU.add).then_inc(tab_step, 1)
                    nc.vector.tensor_copy(meta[:, :, :, P + 1].bitcast(I32), dest[:, :, :]).then_inc(meta_done, 1)
                    dve.wait_ge(rt_step, 5 * g + 5)
                    nc.vector.tensor_tensor(placed[:, :, :, :], oneh[:, :, :, :],
                                            place[:, :, None, :].to_broadcast([P, J, 2, E]), ALU.mult).then_inc(tab_step, 1)
                    dve.wait_ge(tab_step, TABS * g + 1)
                    nc.vector.tensor_tensor(hist[:, :], hist[:, :], seen[:, :], ALU.add).then_inc(tab_step, 1)
                    dve.wait_ge(meta_done, META * g + 1)
                    nc.vector.tensor_scalar(dest[:, :, :], dest[:, :, :], 2.0 * G, None, ALU.add).then_inc(tab_step, 1)
                    dve.wait_ge(tab_step, TABS * g + 2)
                    with nc.allow_low_precision(reason="a row's number, a whole number below 2**24"):
                        nc.vector.tensor_reduce(slot[:, k, :, :], placed[:, :, :, :], AX.X, ALU.add).then_inc(slot_done, 1)

                def weigh(i, c):
                    k, g = c % 2, grp(i, c)
                    meta = rows[:, k, :, :, :]
                    dve.wait_ge(ediff_done, g + 1)
                    nc.vector.tensor_scalar(wsum[:, :], ediff[:, :], 1.0, None, ALU.add).then_inc(wsum_done, 1)
                    dve.wait_ge(wsum_done, g + 1)
                    nc.vector.reciprocal(wfirst[:, :], wsum[:, :]).then_inc(meta_done, 1)
                    dve.wait_ge(meta_done, META * g + 2)
                    nc.vector.tensor_scalar(meta[:, :, 0, P], wfirst[:, :], DOWN, None, ALU.mult).then_inc(meta_done, 1)
                    nc.vector.scalar_tensor_tensor(meta[:, :, 1, P], wfirst[:, :], DOWN, ediff[:, :],
                                                   ALU.mult, ALU.mult).then_inc(meta_done, 1)

                def firststats(b):
                    dve.wait_ge(x_in[b], 16 * (batches[b][1] - batches[b][0]))
                    alone(dve)
                    for t in range(tiles1[b]):
                        ins = nc.vector.bn_stats(bns1[b][:, t, :], acc[:, batches[b][0] * J + t, :])
                    ins.then_inc(first_bn, 1)
                    dve.wait_ge(first_bn, b + 1)
                    alone(dve)
                    for t in range(tiles1[b]):
                        ins = nc.vector.bn_aggr(mv1[b][:, t, :], bns1[b][:, t, :])
                    ins.then_inc(first_mv, 1)

                def stats(i, c):
                    g = grp(i, c)
                    dve.wait_ge(x2_done, 2 * g + 2)
                    ifat(dve, i, c, 1, mv_done, g)
                    alone(dve)
                    for j in range(J):
                        ins = nc.vector.bn_stats(bns[:, j, :], acc[:, g * J + j, :])
                    ins.then_inc(bn_done, 1)
                    dve.wait_ge(bn_done, g + 1)
                    ifat(dve, i, c, 1, ln_step, LNS * g)
                    alone(dve)
                    for j in range(J):
                        ins = nc.vector.bn_aggr(mv[:, j, :], bns[:, j, :])
                    ins.then_inc(mv_done, 1)

                def weights(i, c):
                    for e in experts(i, c):
                        dve.wait_ge(whi_done, e + 1)
                        nc.vector.scalar_tensor_tensor(w1l[:, e * 2 * HR:(e + 1) * 2 * HR], wst[:, e % 2, :], UP,
                                                       w1h[:, e * 2 * HR:(e + 1) * 2 * HR],
                                                       ALU.mult, ALU.subtract).then_inc(wlo_done, 1)

                def second(i, c):
                    k, g = c % 2, grp(i, c)
                    dve.wait_ge(lo_done, g + 1)
                    nc.vector.tensor_copy(rows[:, k, :, 1, 0:C], rows[:, k, :, 0, 0:C]).then_inc(rows_done, 1)

                def body(i, c):
                    begin, end, ffn, tail = stages(i, c)
                    s = grp(i, c)
                    if end:
                        quotient(i, c - 1, 1)
                    if begin:
                        ekv(i, c, 0)
                    if end:
                        refine(i, c - 1, 1)
                    if tail:
                        addffn(i, c - 3, 0)
                    if end:
                        add(i, c - 1, 1)
                        stats(i, c - 1)
                    if begin:
                        scan(i, c, 0)
                    if ffn:
                        logits(i, c - 2)
                    if begin:
                        cutoff(i, c, 0)
                    if isinstance(i, int) and s == 0:
                        firststats(0)
                    if ffn:
                        best(i, c - 2)
                    if begin:
                        ekv(i, c, 1)
                    if ffn:
                        which(i, c - 2)
                    if begin:
                        scan(i, c, 1)
                    if ffn:
                        assign(i, c - 2)
                    if begin:
                        cutoff(i, c, 1)
                        den(i, c, 0)
                    if isinstance(i, int) and s in (0, 1):
                        firststats(s + 1)
                    if ffn:
                        weigh(i, c - 2)
                    if end:
                        second(i, c - 1)
                    if begin:
                        quotient(i, c, 0)
                        refine(i, c, 0)
                        add(i, c, 0)
                    if tail and not begin:
                        addffn(i, c - 3, 1)
                    if isinstance(i, int) and s == NG + 1:
                        table()
                    if not begin:
                        weights(i, c)
                    if ffn:
                        geglu(i, c - 2, 0, 0)
                        geglu(i, c - 2, 0, 1)
                    if tail and begin:
                        addffn(i, c - 3, 1)
                    if begin:
                        den(i, c, 1)
                        weights(i, c)
                    if ffn:
                        geglu(i, c - 2, 1, 0)
                        geglu(i, c - 2, 1, 1)

                def table():
                    n = [TABS * NG]

                    def link(ins):
                        n[0] += 1
                        ins.then_inc(tab_step, 1)
                        dve.wait_ge(tab_step, n[0])

                    def row(k):
                        return tab[:, k, :]

                    def col(k):
                        return tcol[:, k:k + 1]

                    dve.wait_ge(cnt_done, 1)
                    link(nc.vector.tensor_copy(counts[:, :], p_cnt))
                    nc.vector.tensor_tensor(padat[:, :], counts[0:1, :], ebase[0:1, :], ALU.add).then_inc(tab_done, 1)
                    link(nc.vector.tensor_scalar(tabi[:, 0, :], counts[:, :], float(S - 1), None, ALU.add))
                    link(nc.vector.tensor_scalar(tabi[:, 1, :], tabi[:, 0, :], S.bit_length() - 1, None,
                                                 ALU.logical_shift_right))
                    link(nc.vector.tensor_copy(row(0), tabi[:, 1, :]))
                    link(nc.vector.memset(row(2), 1.0))
                    link(nc.vector.tensor_tensor_scan(row(1), row(2), row(0), 0.0, ALU.mult, ALU.add))
                    link(nc.vector.tensor_tensor(row(3), row(1), row(0), ALU.subtract))
                    link(nc.vector.scalar_tensor_tensor(row(4), row(3), -float(S), ebase[:, :], ALU.mult, ALU.add))
                    link(nc.vector.tensor_scalar(row(5), row(1), tileno[:, 0:1], None, ALU.is_le))
                    link(nc.vector.tensor_reduce(col(2), row(5), AX.X, ALU.add))
                    link(nc.vector.tensor_scalar(row(2), eidx[:, :], col(2), None, ALU.is_equal))
                    link(nc.vector.tensor_tensor(row(3), row(2), row(4), ALU.mult))
                    link(nc.vector.tensor_reduce(col(3), row(3), AX.X, ALU.add))
                    link(nc.vector.scalar_tensor_tensor(col(4), tileno[:, :], float(S), col(3), ALU.mult, ALU.add))
                    link(nc.vector.tensor_scalar(col(5), tileno[:, :], -float(S), float(PADROW), ALU.mult, ALU.add))
                    link(nc.vector.tensor_scalar(col(0), col(2), float(E), None, ALU.is_ge))
                    link(nc.vector.scalar_tensor_tensor(col(1), col(5), col(0), col(4), ALU.mult, ALU.add))
                    nc.vector.tensor_scalar(col(0), col(2), float(E - 1), None, ALU.min).then_inc(tcol_done, 1)
                    dve.wait_ge(trow_done, 1)
                    for table_, a in ((tileE, 0), (tileR, P)):
                        nc.vector.tensor_copy(table_[:, :, 0:W], p_tile[:, a:a + NT].rearrange(
                            "p (r k) -> p r k", k=W)).then_inc(tab_done, 1)
                        nc.vector.tensor_copy(table_[:, 1:NT // W, W], p_tile[:, a + W - 1:a + NT - 1:W]).then_inc(tab_done, 1)
                    nc.vector.memset(tileE[:, 0, W:W + 1], 0).then_inc(tab_done, 1)
                steps(dve, body)

                for h in range(2):
                    addffn(NG // 2 - 1, 1, h)

            @block.tensor
            def _(pe):
                pe.wait_ge(sw_in, SW_LOADS)
                pe.wait_ge(pool_const, POOL_CONSTS)
                nc.tensor.transpose(p_vec, vrow[:, :], identf[0:NB, 0:NB]).then_inc(pe_const, 1)
                pe.wait_ge(act_const, 4)
                pe.wait_ge(dve_const, DVE_CONSTS)

                def ctxT(i, c, h):
                    k, g = c % 2, grp(i, c)
                    if h == 0:
                        pe.wait_ge(ctx_ld[k], 16 * turn(i, c))
                    if not (isinstance(i, int) and g == 0 and h == 0):
                        pe.wait_ge(ekv_done, 2 * g + h)
                    if h == 0:
                        ifat(pe, i, c, 3, gl_done, 4 * (g - 2))
                    for j in range(JH):
                        ins = nc.tensor.transpose(p_ct[:, j * P:(j + 1) * P], ct[:, k, h * JH + j, :], identf[:, :])
                    ins.then_inc(ctxT_done, 1)

                def sums(i, c, h, v):
                    k, g = c % 2, grp(i, c)
                    n = 2 * g + h
                    bank, done, used = ((p_num, np_done, quo_done), (p_den, dp_done, den_done))[v]
                    pe.wait_ge(scan_done, n + 1)
                    if not (isinstance(i, int) and n == 0):
                        pe.wait_ge(used, n)
                    for j in range(JH):
                        to = bank[:, j * P:(j + 1) * P]
                        a = v * H + j * P
                        nc.tensor.matmul(to, fw[:, h, a:a + P], identf[:, :], start=True, stop=False)
                        nc.tensor.matmul(to, bw[:, h, a + 1:a + 1 + P], identf[:, :], start=False, stop=False)
                        ins = nc.tensor.matmul(to, ek[:, k, h, v, j * P:(j + 1) * P], diagu[:, :],
                                               start=False, stop=True)
                    ins.then_inc(done, 1)

                def turnx(i, c, h):
                    k, g = c % 2, grp(i, c)
                    pe.wait_ge(lo_done, g + 1)
                    if not (isinstance(i, int) and g == 0 and h == 0):
                        pe.wait_ge(xT_done, 2 * g + h)
                    ifat(pe, i, c, 1, hid_done, 4 * g)
                    for l in range(2):
                        for j in range(JH):
                            ins = nc.tensor.transpose(
                                p_xT[:, l, j * P:(j + 1) * P],
                                rows[:, k, h * JH + j, 0, l * (C // 2):(l + 1) * (C // 2)].bitcast(F16), identh[:, :])
                    ins.then_inc(xTp_done, 1)

                def router(i, c):
                    g = grp(i, c)
                    pe.wait_ge(xT_done, 2 * g + 2)
                    ifat(pe, i, c, 1, slot_done, g)
                    for j in range(J):
                        xh = xT[:, j // JH, 0, (j % JH) * P:(j % JH + 1) * P]
                        xl = xT[:, j // JH, 1, (j % JH) * P:(j % JH + 1) * P]
                        to = p_lg[:, j * E:(j + 1) * E]
                        nc.tensor.matmul(to, xh, wrh[:, :], start=True, stop=False)
                        nc.tensor.matmul(to, xh, wrl[:, :], start=False, stop=False)
                        ins = nc.tensor.matmul(to, xl, wrh[:, :], start=False, stop=True)
                    ins.then_inc(lgp_done, 1)

                def prefix(i, c):
                    g = grp(i, c)
                    pe.wait_ge(both_done, g + 1)
                    ifat(pe, i, c, 1, slot_done, g)
                    nc.tensor.matmul(p_pf, before[:, :], both[:, :, :].rearrange("p j e -> p (j e)"), start=True, stop=False)
                    for j in range(J - 1):
                        nc.tensor.matmul(p_pf[:, (j + 1) * E:J * E], ones[:, :],
                                         both[:, j:j + 1, :].to_broadcast([P, J - 1 - j, E]), start=False, stop=False)
                    nc.tensor.matmul(p_pf, ones[:, :], hist[:, None, :].to_broadcast([P, J, E]),
                                     start=False, stop=True).then_inc(pf_done, 1)

                def up(bank, off, i, c, h, f):
                    cols = slice(off + f * P, off + (f + 1) * P)
                    nc.tensor.matmul(bank[:, :], s1h[:, cols], xT[:, h, 0, :], start=True, stop=False)
                    nc.tensor.matmul(bank[:, :], s1h[:, cols], xT[:, h, 1, :], start=False, stop=False)
                    return nc.tensor.matmul(bank[:, :], s1l[:, cols], xT[:, h, 0, :], start=False, stop=True)

                def upg(i, c, h, f):
                    g = grp(i, c)
                    n = 4 * g + 2 * h + f
                    pe.wait_ge(xT_done, 2 * g + h + 1)
                    if f == 1 and h == 0:
                        pe.wait_ge(ekv_done, min(2 * (g + 2) + 2, 2 * NG) if isinstance(i, int) else 2 * (g + 2) + 2)
                    if not (isinstance(i, int) and n <= 1):
                        pe.wait_ge(gl_done, n - 1)
                    up((p_g, p_ct)[f], HS, i, c, h, f).then_inc(upg_done, 1)

                def upa(i, c, h, f):
                    g = grp(i, c)
                    n = 4 * g + 2 * h + f
                    pe.wait_ge(xT_done, 2 * g + 2)
                    if not (isinstance(i, int) and n <= 1):
                        pe.wait_ge(hid_done, n - 1)
                    up((p_a, p_xTf)[f], 0, i, c, h, f).then_inc(upa_done, 1)

                def down(i, c, h):
                    g = grp(i, c)
                    pe.wait_ge(hid_done, 4 * g + 2 * h + 2)
                    if not (isinstance(i, int) and g == 0 and h == 0):
                        pe.wait_ge(acc_done, 2 * g + h)
                    for j in range(JH):
                        to = p_y[:, j * P:(j + 1) * P]
                        for f in range(KS):
                            nc.tensor.matmul(to, hid[:, h, f, j * P:(j + 1) * P], s2[:, f, :], start=(f == 0), stop=False)
                        ins = nc.tensor.matmul(to, ones[0:3, :], b2s[:, E * C:(E + 1) * C], start=False, stop=True)
                    ins.then_inc(yp_done, 1)

                def body(i, c):
                    begin, end, ffn, tail = stages(i, c)
                    if isinstance(i, int) and grp(i, c) == 3:
                        pe.wait_ge(parts_in, 16)
                    if begin:
                        ctxT(i, c, 0)
                    if ffn:
                        turnx(i, c - 2, 0)
                    if tail:
                        down(i, c - 3, 0)
                    if ffn:
                        turnx(i, c - 2, 1)
                    if begin:
                        ctxT(i, c, 1)
                    if ffn:
                        router(i, c - 2)
                        upg(i, c - 2, 0, 0)
                        upa(i, c - 2, 0, 0)
                    if tail:
                        down(i, c - 3, 1)
                    if begin:
                        sums(i, c, 0, 1)
                    if ffn:
                        prefix(i, c - 2)
                    if begin:
                        sums(i, c, 0, 0)
                    if ffn:
                        upg(i, c - 2, 0, 1)
                        upa(i, c - 2, 0, 1)
                    if isinstance(i, int) and grp(i, c) == NG + 1:
                        table()
                    if begin:
                        sums(i, c, 1, 1)
                    if ffn:
                        upg(i, c - 2, 1, 0)
                    if begin:
                        sums(i, c, 1, 0)
                    if ffn:
                        upg(i, c - 2, 1, 1)
                        upa(i, c - 2, 1, 0)
                        upa(i, c - 2, 1, 1)

                def table():
                    pe.wait_ge(tab_step, TABS * NG)
                    nc.tensor.matmul(p_cnt, ones[:, :], hist[:, :], start=True, stop=True).then_inc(cnt_done, 1)
                    pe.wait_ge(tcol_done, 1)
                    for k in range(2):
                        ins = nc.tensor.transpose(p_tile[:, k * P:(k + 1) * P], tcol[:, k:k + 1], identf[:, :])
                    ins.then_inc(trow_done, 1)
                steps(pe, body)
                for h in range(2):
                    down(NG // 2 - 1, 1, h)

        def tiles(eng, kind, table, low, high, body):
            def round_of(i, first, last):
                count = W + 1 if kind == PE else W
                entries = table[0:1, i, 0:count] if isinstance(i, int) else \
                    table[0:1, bass.ds(i, 1), 0:count].rearrange("p r k -> p (r k)")
                values = nc.values_load_multi_w_load_instructions(
                    entries, engines=[kind], min_val=low, max_val=high,
                    skip_runtime_bounds_check_because="the table is made of numbers in this range")[1]
                which = {-1: values[-1], **dict(enumerate(values[:W]))}
                for c in range(W):
                    body(i, c, which, first, last)

            round_of(0, True, False)
            round_of(1, False, False)
            with eng.Fori(2, NT // W - 1) as i:
                round_of(i, False, False)
            round_of(NT // W - 1, False, True)
        assert NT % W == 0

        with nc.Block() as block:
            @block.sync
            def _(sp):
                def body(i, c, row, first, last):
                    if not first:
                        sp.wait_ge(t_out[c], 32 * i)
                    sp.dma_start(tin[:, c, :, :], sorted_d[bass.ds(row[c], S), :].rearrange("(h p) r -> p h r", p=P)
                                 ).then_inc(t_in[c], 16)
                tiles(sp, mybir.EngineType.SP, tileR, 0, PADROW, body)

            @block.tensor
            def _(pe):
                def turnx(i, c):
                    t = W * i + c
                    pe.wait_ge(t_in[c % W], 16 * (i + c // W + 1))
                    if not (isinstance(i, int) and t == 0):
                        pe.wait_ge(tx_done, t)
                    for l in range(2):
                        for h in range(2):
                            ins = nc.tensor.transpose(p_tx[:, 0, l * S + h * P:l * S + (h + 1) * P],
                                                      tin[:, c % W, h, l * (C // 2):(l + 1) * (C // 2)].bitcast(F16),
                                                      identh[:, :])
                    ins.then_inc(txp_done, 1)

                def up(i, c, k, e, first):
                    t = W * i + c
                    if k == 0:
                        pe.wait_ge(tx_done, t + 1)
                    if not (first and c == 0):
                        pe.wait_ge(thid_done, KR * (t - 1) + k + 1)
                    xh, xl = txT[:, c, 0, :], txT[:, c, 1, :]
                    for bank, off, done in ((p_tg[k], KR + k, tg_done), (p_ta[k], k, ta_done)):
                        to = bank[:, 0:S]
                        cols = bass.ds(e * (2 * HR) + off * P, P)
                        nc.tensor.matmul(to, w1h[:, cols], xh, start=True, stop=False)
                        nc.tensor.matmul(to, w1h[:, cols], xl, start=False, stop=False)
                        nc.tensor.matmul(to, w1l[:, cols], xh, start=False, stop=True).then_inc(done, 1)

                def down(i, c, e):
                    t = W * i + c
                    pe.wait_ge(thid_done, KR * t + KR)
                    if not (isinstance(i, int) and t == 0):
                        pe.wait_ge(ty_done, t)
                    for h in range(2):
                        to = p_ty[:, h * P:(h + 1) * P]
                        for k in range(KR):
                            nc.tensor.matmul(to, thid[:, c % W, k, h * P:(h + 1) * P],
                                             w2[:, bass.ds(e * KR + k, 1), :], start=(k == 0), stop=False)
                        ins = nc.tensor.matmul(to, ones[0:3, :], b2s[:, bass.ds(e * C, C)], start=False, stop=True)
                    ins.then_inc(typ_done, 1)

                def body(i, c, expert, first, last):
                    if first and c == 0:
                        turnx(i, 0)
                        turnx(i, 1)
                    e = expert[c]
                    up(i, c, 0, e, first)
                    up(i, c, 1, e, first)
                    if not (first and c == 0):
                        down(i, c - 1, expert[c - 1])
                    if not (last and c + 2 >= W):
                        turnx(i, c + 2)
                    up(i, c, 2, e, first)
                    if last and c == W - 1:
                        down(i, c, e)
                tiles(pe, PE, tileE, 0, E - 1, body)

            @block.scalar
            def _(act):
                def outx(i, c, first):
                    t = W * i + c
                    act.wait_ge(txp_done, t + 1)
                    if not (first and c < W):
                        act.wait_ge(ta_done, KR * (t - W) + KR)
                    nc.scalar.activation(txT[:, c % W, :, :], p_tx[:, 0, 0:2 * S].rearrange("p (l n) -> p l n", l=2),
                                         ACT.Copy).then_inc(tx_done, 1)

                def body(i, c, expert, first, last):
                    t, e = W * i + c, expert[c]
                    if first and c == 0:
                        outx(i, 0, first)
                        outx(i, 1, first)
                    for k in range(KR):
                        act.wait_ge(tg_done, KR * t + k + 1)
                        if not (first and c == 0):
                            act.wait_ge(thid_done, KR * (t - 1) + k + 1)
                        alone(act)
                        nc.scalar.activation(tgl[:, k, :], p_tg[k][:, 0:S], ACT.Gelu, scale=DOWN,
                                             bias=vcol[:, bass.ds(e * (2 * KR) + KR + k, 1)]).then_inc(tgl_done, 1)
                        if k == 1 and not (last and c + 2 >= W):
                            outx(i, c + 2, first)
                tiles(act, mybir.EngineType.Activation, tileE, 0, E - 1, body)

            @block.vector
            def _(dve):
                def outy(i, c, first):
                    t = W * i + c
                    dve.wait_ge(typ_done, t + 1)
                    if not (isinstance(i, int) and t < W):
                        dve.wait_ge(t_out[c % W], 32 * (i + c // W))
                    for h in range(2):
                        ins = nc.vector.tensor_scalar(tyo[:, c % W, h, :], p_ty[:, h * P:(h + 1) * P],
                                                      tin[:, c % W, h, P:P + 1], None, ALU.mult)
                    ins.then_inc(ty_done, 1)

                def body(i, c, expert, first, last):
                    t, e = W * i + c, expert[c]
                    for k in range(KR):
                        dve.wait_ge(ta_done, KR * t + k + 1)
                        dve.wait_ge(tgl_done, KR * t + k + 1)
                        if not first:
                            dve.wait_ge(typ_done, t - W + 1)
                        nc.vector.scalar_tensor_tensor(thid[:, c, k, :], p_ta[k][:, 0:S],
                                                       vup[:, bass.ds(e * (2 * KR) + k, 1)], tgl[:, k, :],
                                                       ALU.add, ALU.mult).then_inc(thid_done, 1)
                        if k == 1 and not (first and c == 0):
                            outy(i, c - 1, first)
                    if last and c == W - 1:
                        outy(i, c, first)
                tiles(dve, mybir.EngineType.DVE, tileE, 0, E - 1, body)

            @block.gpsimd
            def _(pool):
                def body(i, c, first, last):
                    pool.wait_ge(ty_done, W * i + c + 1)
                    alone(pool)
                    for h in range(2):
                        pool.indirect_dma_start(
                            out=y_d, out_offset=bass.IndirectOffsetOnAxis(ap=tin[:, c, h, P + 1:P + 2].bitcast(U32), axis=0),
                            in_=tyo[:, c, h, :], in_offset=None, bounds_check=2 * N - 1, oob_is_err=False
                        ).then_inc(t_out[c], 16)
                for c in range(W):
                    body(0, c, True, False)
                with pool.Fori(1, NT // W) as i:
                    for c in range(W):
                        body(i, c, False, False)
                for c in range(W):
                    pool.wait_ge(t_out[c], 32 * (NT // W))

        with nc.Block() as block:
            @block.sync
            def _(sp):
                def load(i, c):
                    g = grp(i, c)
                    if not (isinstance(i, int) and g < 2):
                        sp.wait_ge(sum_done, g - 1)
                    sp.dma_start(ybuf[:, c % 2, :, :, :].rearrange("p j k c -> p j (k c)"),
                                 yg_d[g, :, :, :]).then_inc(y_in[c % 2], 16)

                def store(i, c):
                    g = grp(i, c)
                    sp.wait_ge(sum_done, g + 1)
                    sp.dma_start(og_d[g, :, :, :], acc[:, bass.ds(g * J, J), :]).then_inc(out_done, 16)
                load(0, 0)
                load(0, 1)
                with sp.Fori(1, NG // 2) as i:
                    for c in range(2):
                        load(i, c)
                        store(i, c - 2)
                store(NG // 2 - 1, 0)
                store(NG // 2 - 1, 1)
                sp.wait_ge(out_done, 16 * NG)

            @block.vector
            def _(dve):
                with dve.Fori(0, NG // 2) as i:
                    for c in range(2):
                        g = grp(i, c)
                        at = acc[:, bass.ds(g * J, J), :]
                        dve.wait_ge(y_in[c], 16 * (i + 1))
                        nc.vector.tensor_tensor(at, at, ybuf[:, c, :, 0, :], ALU.add).then_inc(add1, 1)
                        dve.wait_ge(add1, g + 1)
                        nc.vector.tensor_tensor(at, at, ybuf[:, c, :, 1, :], ALU.add).then_inc(sum_done, 1)


_INS = ['x', 'ctx_1024', 'L0_xattn_w', 'L0_xattn_u', 'L0_ffn_Ws1', 'L0_ffn_bs1', 'L0_ffn_Ws2', 'L0_ffn_bs2',
        'L0_ffn_We1', 'L0_ffn_be1', 'L0_ffn_We2', 'L0_ffn_be2', 'L0_ffn_Wr', 'L0_ffn_br']


def kernel(**inputs):
    import numpy as _np
    import concourse.bacc as _bacc
    from concourse import mybir as _mybir
    from concourse.bass_utils import run_bass_kernel_spmd as _run

    nc = _bacc.Bacc("TRN2", target_bir_lowering=False, num_devices=1)
    arrays, args = {}, []
    for name in _INS:
        a = _np.ascontiguousarray(inputs[name])
        arrays[f"in_{name}_dram"] = a
        args.append(nc.dram_tensor(f"in_{name}_dram", a.shape, _mybir.dt.from_np(a.dtype), kind="ExternalInput").ap())
    shape = inputs['x'].shape
    args.append(nc.dram_tensor("out_0_dram", shape, _mybir.dt.float32, kind="ExternalOutput").ap())
    xattn_ffn_kernel(nc, *args)
    r = _run(nc, [arrays], core_ids=[0])
    return r.results[0]["out_0_dram"]
```
